# Optimizing a Trainium2 kernel written in Bass

```python
import numpy as np
import jax
import jax.numpy as jnp

def _softmax(x, axis=-1):
    return jax.nn.softmax(x, axis=axis)

def _gelu(x):
    return jax.nn.gelu(x, approximate=True)

def _silu(x):
    return jax.nn.silu(x)

def _sigmoid(x):
    return jax.nn.sigmoid(x)

def _layernorm(x, axis=-1, eps=1e-05):
    m = jnp.mean(x, axis=axis, keepdims=True)
    v = jnp.var(x, axis=axis, keepdims=True)
    return (x - m) / jnp.sqrt(v + eps)

def _scatter_add(tgt, idx, src, axis=0):
    return tgt.at[idx].add(src)

def _segment_sum(src, seg, n):
    return jax.ops.segment_sum(src, seg, n)
kernel_name = 'mk_gnn_ffn_d4_gnn_r32_64c004'

def setup_inputs(seed: int=0):
    np.random.seed(seed)
    _w = jnp.asarray

    def _rec_inputs():
        import jax
        import jax.numpy as jnp
        _gk = jax.random.key(seed)
        x = -0.0003713 + 1 * jax.random.normal(jax.random.fold_in(_gk, 1), (3125, 256), jnp.float32)
        src = jax.random.randint(jax.random.fold_in(_gk, 2), (50000,), 0, 3125, jnp.int32)
        dst = jax.random.randint(jax.random.fold_in(_gk, 3), (50000,), 0, 3125, jnp.int32)
        _o = jnp.argsort(dst, stable=True)
        src = src[_o]
        dst = dst[_o]
        edge_attr_4 = 0.000126197 + 0.999763 * jax.random.normal(jax.random.fold_in(_gk, 12), (50000, 4), jnp.float32)
        edge_attr_8 = jax.random.uniform(jax.random.fold_in(_gk, 13), (50000, 8), jnp.float32, 0.0, 1)
        return (x, src, dst, edge_attr_4, edge_attr_8)
    x, src, dst, edge_attr_4, edge_attr_8 = _rec_inputs()

    def _L0_gnn_setup():
        import jax, jax.numpy as jnp
        import numpy as np
        N = 50000
        E_RAND = 25000
        F_IN = 256
        F_OUT = 256
        ALPHA = 0.2
        key = jax.random.key(seed)
        k1, k2, k3, k4 = jax.random.split(key, 4)
        x = jax.random.normal(k1, (N, F_IN), dtype=jnp.float32)
        edge_rand = jax.random.randint(k2, (2, E_RAND), 0, N)
        loops = jnp.arange(N)
        edge = jnp.concatenate([edge_rand, jnp.stack([loops, loops])], axis=1)
        W = jax.random.normal(k3, (F_IN, F_OUT), dtype=jnp.float32) * 0.05
        a = jax.random.normal(k4, (2 * F_OUT,), dtype=jnp.float32) * 0.05
        return {'x': x, 'edge': edge, 'W': W, 'a': a}
    _L0_gnn_all = _L0_gnn_setup()
    _L0_gnn_in = {k: v for k, v in _L0_gnn_all.items() if k in ('W', 'a')}
    del _L0_gnn_all

    def _L0_ffn_setup():
        import jax, jax.numpy as jnp
        import numpy as np
        B, K, D = (512, 16, 256)
        E = 32
        H = int(D * 0.25)
        key = jax.random.key(seed)
        ks = jax.random.split(key, 7)
        d_rs = D ** (-0.5)
        h_rs = H ** (-0.5)
        x = jax.random.normal(ks[0], (B, K, D), dtype=jnp.float32)
        router_w = jax.random.uniform(ks[1], (E, D), jnp.float32, -d_rs, d_rs)
        router_b = jax.random.uniform(ks[2], (E,), jnp.float32, -d_rs, d_rs)
        W1 = jax.random.uniform(ks[3], (E, D, H), jnp.float32, -h_rs, h_rs)
        b1 = jax.random.uniform(ks[4], (E, H), jnp.float32, -h_rs, h_rs)
        W2 = jax.random.uniform(ks[5], (E, H, D), jnp.float32, -d_rs, d_rs)
        b2 = jax.random.uniform(ks[6], (E, D), jnp.float32, -d_rs, d_rs)
        return {'x': x, 'router_w': router_w, 'router_b': router_b, 'W1': W1, 'b1': b1, 'W2': W2, 'b2': b2}
    _L0_ffn_all = _L0_ffn_setup()
    _L0_ffn_in = {k: v for k, v in _L0_ffn_all.items() if k in ('router_w', 'router_b', 'W1', 'b1', 'W2', 'b2')}
    del _L0_ffn_all

    def _L1_gnn_setup():
        import jax, jax.numpy as jnp
        import numpy as np
        N_NODES = 625
        N_EDGES = 10000
        MUL = 64
        NUM_BASIS = 8
        INV_SQRT3 = 0.5773502691896258
        EPS = 1e-05
        key = jax.random.key(seed)
        k = jax.random.split(key, 16)
        return {'node_hiddens': jax.random.normal(k[0], (N_NODES, 4 * MUL), dtype=jnp.float32), 'edge_attr': jax.random.uniform(k[1], (N_EDGES, NUM_BASIS), dtype=jnp.float32), 'edge_sh': jax.random.normal(k[2], (N_EDGES, 4), dtype=jnp.float32), 'w1_s': jax.random.normal(k[3], (MUL, MUL), dtype=jnp.float32), 'w1_v': jax.random.normal(k[4], (MUL, MUL), dtype=jnp.float32), 'wsc_s': jax.random.normal(k[5], (MUL, MUL), dtype=jnp.float32), 'wsc_v': jax.random.normal(k[6], (MUL, MUL), dtype=jnp.float32), 'w2_s': jax.random.normal(k[7], (2 * MUL, MUL), dtype=jnp.float32), 'w2_v': jax.random.normal(k[8], (2 * MUL, MUL), dtype=jnp.float32), 'fc_w1': jax.random.normal(k[9], (NUM_BASIS, 64), dtype=jnp.float32), 'fc_w2': jax.random.normal(k[10], (64, 64), dtype=jnp.float32), 'fc_w3': jax.random.normal(k[11], (64, 4 * MUL), dtype=jnp.float32), 'g_s': jnp.ones((MUL,), dtype=jnp.float32), 'g_v': jnp.ones((MUL,), dtype=jnp.float32), 'edge_index': jax.random.randint(k[12], (2, N_EDGES), 0, N_NODES)}
    _L1_gnn_all = _L1_gnn_setup()
    _L1_gnn_in = {k: v for k, v in _L1_gnn_all.items() if k in ('w1_s', 'w1_v', 'wsc_s', 'wsc_v', 'w2_s', 'w2_v', 'fc_w1', 'fc_w2', 'fc_w3', 'g_s', 'g_v')}
    del _L1_gnn_all

    def _L1_ffn_setup():
        import jax, jax.numpy as jnp
        import numpy as np
        E, D, H, TOP_K = (6, 256, 256, 2)
        ROUTER_H = D // 2
        key = jax.random.key(seed)
        ks = jax.random.split(key, 12)
        s = 1.0 / np.sqrt(D)
        sh = 1.0 / np.sqrt(H)
        sr = 1.0 / np.sqrt(ROUTER_H)
        return {'features': jax.random.normal(ks[0], (8, 128, D), dtype=jnp.float32), 'router_w1': jax.random.uniform(ks[1], (D, ROUTER_H), jnp.float32, -s, s), 'router_b1': jnp.zeros((ROUTER_H,), jnp.float32), 'router_w2': jax.random.uniform(ks[2], (ROUTER_H, E), jnp.float32, -sr, sr), 'router_b2': jnp.zeros((E,), jnp.float32), 'expert_w1': jax.random.uniform(ks[3], (E, D, H), jnp.float32, -s, s), 'expert_b1': jnp.zeros((E, H), jnp.float32), 'expert_w2': jax.random.uniform(ks[4], (E, H, H), jnp.float32, -sh, sh), 'expert_b2': jnp.zeros((E, H), jnp.float32), 'expert_w3': jax.random.uniform(ks[5], (E, H, D), jnp.float32, -sh, sh), 'expert_b3': jnp.zeros((E, D), jnp.float32)}
    _L1_ffn_all = _L1_ffn_setup()
    _L1_ffn_in = {k: v for k, v in _L1_ffn_all.items() if k in ('router_w1', 'router_b1', 'router_w2', 'router_b2', 'expert_w1', 'expert_b1', 'expert_w2', 'expert_b2', 'expert_w3', 'expert_b3')}
    del _L1_ffn_all

    def _L2_gnn_setup():
        import jax, jax.numpy as jnp
        import numpy as np
        N_NODES = 3125
        N_EDGES = 50000
        HID = 256
        HEADS = 4
        HEAD_DIM = HID // HEADS
        EPS = 1e-05

        def _layernorm(x, g, b):
            mu = jnp.mean(x, axis=-1, keepdims=True)
            var = jnp.mean(jnp.square(x - mu), axis=-1, keepdims=True)
            return (x - mu) * jax.lax.rsqrt(var + EPS) * g + b
        key = jax.random.key(seed)
        ks = jax.random.split(key, 16)
        s = 0.05
        inp = {'h': jax.random.normal(ks[0], (N_NODES, HID), jnp.float32), 'src': jax.random.randint(ks[1], (N_EDGES,), 0, N_NODES, jnp.int32), 'dst': jax.random.randint(ks[2], (N_EDGES,), 0, N_NODES, jnp.int32), 'Wq': jax.random.normal(ks[3], (HID, HID), jnp.float32) * s, 'bq': jnp.zeros((HID,), jnp.float32), 'Wk': jax.random.normal(ks[4], (HID, HID), jnp.float32) * s, 'bk': jnp.zeros((HID,), jnp.float32), 'Wv': jax.random.normal(ks[5], (HID, HID), jnp.float32) * s, 'bv': jnp.zeros((HID,), jnp.float32), 'Wo': jax.random.normal(ks[6], (HID, HID), jnp.float32) * s, 'bo': jnp.zeros((HID,), jnp.float32), 'W1': jax.random.normal(ks[7], (HID, 2 * HID), jnp.float32) * s, 'b1': jnp.zeros((2 * HID,), jnp.float32), 'W2': jax.random.normal(ks[8], (2 * HID, HID), jnp.float32) * s, 'b2': jnp.zeros((HID,), jnp.float32), 'g1': jnp.ones((HID,), jnp.float32), 'be1': jnp.zeros((HID,), jnp.float32), 'g2': jnp.ones((HID,), jnp.float32), 'be2': jnp.zeros((HID,), jnp.float32)}
        return inp
    _L2_gnn_all = _L2_gnn_setup()
    _L2_gnn_in = {k: v for k, v in _L2_gnn_all.items() if k in ('Wq', 'bq', 'Wk', 'bk', 'Wv', 'bv', 'Wo', 'bo', 'W1', 'b1', 'W2', 'b2', 'g1', 'be1', 'g2', 'be2')}
    del _L2_gnn_all

    def _L2_ffn_setup():
        import jax, jax.numpy as jnp
        import numpy as np
        BN_EPS = 0.001

        def _bn(h, g, b, m, v):
            return g * (h - m) * jax.lax.rsqrt(v + BN_EPS) + b
        key = jax.random.key(seed)
        ks = jax.random.split(key, 8)
        B, F, Df = (256, 64, 256)
        E, H, D = (8, 256, 256)
        s1 = 1.0 / np.sqrt(Df)
        s2 = 1.0 / np.sqrt(H)
        return {'x': jax.random.normal(ks[0], (B, F, Df), jnp.float32), 'Wr': jax.random.normal(ks[1], (Df, E), jnp.float32) * s1, 'br': jnp.zeros((E,), jnp.float32), 'W1': jax.random.normal(ks[2], (E, Df, H), jnp.float32) * s1, 'b1': jnp.zeros((E, H), jnp.float32), 'g1': jnp.ones((E, H), jnp.float32), 'be1': jnp.zeros((E, H), jnp.float32), 'm1': jnp.zeros((E, H), jnp.float32), 'v1': jnp.ones((E, H), jnp.float32), 'W2': jax.random.normal(ks[3], (E, H, H), jnp.float32) * s2, 'b2': jnp.zeros((E, H), jnp.float32), 'g2': jnp.ones((E, H), jnp.float32), 'be2': jnp.zeros((E, H), jnp.float32), 'm2': jnp.zeros((E, H), jnp.float32), 'v2': jnp.ones((E, H), jnp.float32), 'Wo': jax.random.normal(ks[4], (E, H, D), jnp.float32) * s2, 'bo': jnp.zeros((E, D), jnp.float32)}
    _L2_ffn_all = _L2_ffn_setup()
    _L2_ffn_in = {k: v for k, v in _L2_ffn_all.items() if k in ('Wr', 'br', 'W1', 'b1', 'g1', 'be1', 'm1', 'v1', 'W2', 'b2', 'g2', 'be2', 'm2', 'v2', 'Wo', 'bo')}
    del _L2_ffn_all

    def _L3_gnn_setup():
        import jax, jax.numpy as jnp
        import numpy as np
        NEG = -1000.0
        SLOPE = 0.01
        N_NODES, N_EDGES, D_IN, D_OUT, N_HEADS = (3125, 50000, 256, 64, 4)
        key = jax.random.key(seed)
        k0, k1, k2, k3, k4 = jax.random.split(key, 5)
        h = jax.random.normal(k0, (N_NODES, D_IN), jnp.float32)
        src = jax.random.randint(k1, (N_EDGES,), 0, N_NODES)
        dst = jax.random.randint(k2, (N_EDGES,), 0, N_NODES)
        W = jax.random.normal(k3, (N_HEADS, D_IN, D_OUT), jnp.float32) / np.sqrt(D_IN)
        att = jax.random.normal(k4, (N_HEADS, 2 * D_OUT), jnp.float32) / np.sqrt(2.0 * D_OUT)
        return {'h': h, 'W': W, 'att': att, 'src': src, 'dst': dst}
    _L3_gnn_all = _L3_gnn_setup()
    _L3_gnn_in = {k: v for k, v in _L3_gnn_all.items() if k in ('W', 'att')}
    del _L3_gnn_all

    def _L3_ffn_setup():
        import jax, jax.numpy as jnp
        import numpy as np
        NUM_EXPERTS = 8
        TOP_K = 2
        B, S, D = (8, 256, 256)

        def _moe(tokens, router_w, w1, b1, w2, b2):
            N = tokens.shape[0]
            E = router_w.shape[0]
            logits = tokens.astype(jnp.float32) @ router_w.astype(jnp.float32).T
            probs = jax.nn.softmax(logits, axis=-1)
            rw, re = jax.lax.top_k(probs, TOP_K)
            if TOP_K > 1:
                rw = rw / jnp.maximum(rw.sum(-1, keepdims=True), 1e-12)
            rw = rw.astype(tokens.dtype)
            combine = jnp.zeros((N, E), tokens.dtype).at[jnp.arange(N)[:, None], re].set(rw)
            out = tokens
            for e in range(E):
                h = jax.nn.gelu(tokens @ w1[e] + b1[e], approximate=False)
                y = h @ w2[e] + b2[e]
                out = out + combine[:, e:e + 1] * y
            return out
        key = jax.random.key(seed)
        ks = jax.random.split(key, 4)
        scale = 1.0 / np.sqrt(D).astype(np.float32)
        return {'input_embeddings': jax.random.normal(ks[0], (B, S, D), jnp.float32), 'router_w': jax.random.normal(ks[1], (NUM_EXPERTS, D), jnp.float32) * scale, 'w1': jax.random.normal(ks[2], (NUM_EXPERTS, D, D), jnp.float32) * scale, 'b1': jnp.zeros((NUM_EXPERTS, D), jnp.float32), 'w2': jax.random.normal(ks[3], (NUM_EXPERTS, D, D), jnp.float32) * scale, 'b2': jnp.zeros((NUM_EXPERTS, D), jnp.float32)}
    _L3_ffn_all = _L3_ffn_setup()
    _L3_ffn_in = {k: v for k, v in _L3_ffn_all.items() if k in ('router_w', 'w1', 'b1', 'w2', 'b2')}
    del _L3_ffn_all
    return {'x': x, 'src': src, 'dst': dst, 'edge_attr_4': edge_attr_4, 'edge_attr_8': edge_attr_8, 'L0_gnn_W': _L0_gnn_in['W'], 'L0_gnn_a': _L0_gnn_in['a'], 'L0_ffn_router_w': _L0_ffn_in['router_w'], 'L0_ffn_router_b': _L0_ffn_in['router_b'], 'L0_ffn_W1': _L0_ffn_in['W1'], 'L0_ffn_b1': _L0_ffn_in['b1'], 'L0_ffn_W2': _L0_ffn_in['W2'], 'L0_ffn_b2': _L0_ffn_in['b2'], 'L1_gnn_w1_s': _L1_gnn_in['w1_s'], 'L1_gnn_w1_v': _L1_gnn_in['w1_v'], 'L1_gnn_wsc_s': _L1_gnn_in['wsc_s'], 'L1_gnn_wsc_v': _L1_gnn_in['wsc_v'], 'L1_gnn_w2_s': _L1_gnn_in['w2_s'], 'L1_gnn_w2_v': _L1_gnn_in['w2_v'], 'L1_gnn_fc_w1': _L1_gnn_in['fc_w1'], 'L1_gnn_fc_w2': _L1_gnn_in['fc_w2'], 'L1_gnn_fc_w3': _L1_gnn_in['fc_w3'], 'L1_gnn_g_s': _L1_gnn_in['g_s'], 'L1_gnn_g_v': _L1_gnn_in['g_v'], 'L1_ffn_router_w1': _L1_ffn_in['router_w1'], 'L1_ffn_router_b1': _L1_ffn_in['router_b1'], 'L1_ffn_router_w2': _L1_ffn_in['router_w2'], 'L1_ffn_router_b2': _L1_ffn_in['router_b2'], 'L1_ffn_expert_w1': _L1_ffn_in['expert_w1'], 'L1_ffn_expert_b1': _L1_ffn_in['expert_b1'], 'L1_ffn_expert_w2': _L1_ffn_in['expert_w2'], 'L1_ffn_expert_b2': _L1_ffn_in['expert_b2'], 'L1_ffn_expert_w3': _L1_ffn_in['expert_w3'], 'L1_ffn_expert_b3': _L1_ffn_in['expert_b3'], 'L2_gnn_Wq': _L2_gnn_in['Wq'], 'L2_gnn_bq': _L2_gnn_in['bq'], 'L2_gnn_Wk': _L2_gnn_in['Wk'], 'L2_gnn_bk': _L2_gnn_in['bk'], 'L2_gnn_Wv': _L2_gnn_in['Wv'], 'L2_gnn_bv': _L2_gnn_in['bv'], 'L2_gnn_Wo': _L2_gnn_in['Wo'], 'L2_gnn_bo': _L2_gnn_in['bo'], 'L2_gnn_W1': _L2_gnn_in['W1'], 'L2_gnn_b1': _L2_gnn_in['b1'], 'L2_gnn_W2': _L2_gnn_in['W2'], 'L2_gnn_b2': _L2_gnn_in['b2'], 'L2_gnn_g1': _L2_gnn_in['g1'], 'L2_gnn_be1': _L2_gnn_in['be1'], 'L2_gnn_g2': _L2_gnn_in['g2'], 'L2_gnn_be2': _L2_gnn_in['be2'], 'L2_ffn_Wr': _L2_ffn_in['Wr'], 'L2_ffn_br': _L2_ffn_in['br'], 'L2_ffn_W1': _L2_ffn_in['W1'], 'L2_ffn_b1': _L2_ffn_in['b1'], 'L2_ffn_g1': _L2_ffn_in['g1'], 'L2_ffn_be1': _L2_ffn_in['be1'], 'L2_ffn_m1': _L2_ffn_in['m1'], 'L2_ffn_v1': _L2_ffn_in['v1'], 'L2_ffn_W2': _L2_ffn_in['W2'], 'L2_ffn_b2': _L2_ffn_in['b2'], 'L2_ffn_g2': _L2_ffn_in['g2'], 'L2_ffn_be2': _L2_ffn_in['be2'], 'L2_ffn_m2': _L2_ffn_in['m2'], 'L2_ffn_v2': _L2_ffn_in['v2'], 'L2_ffn_Wo': _L2_ffn_in['Wo'], 'L2_ffn_bo': _L2_ffn_in['bo'], 'L3_gnn_W': _L3_gnn_in['W'], 'L3_gnn_att': _L3_gnn_in['att'], 'L3_ffn_router_w': _L3_ffn_in['router_w'], 'L3_ffn_w1': _L3_ffn_in['w1'], 'L3_ffn_b1': _L3_ffn_in['b1'], 'L3_ffn_w2': _L3_ffn_in['w2'], 'L3_ffn_b2': _L3_ffn_in['b2']}

def reference(x, src, dst, edge_attr_4, edge_attr_8, L0_gnn_W, L0_gnn_a, L0_ffn_router_w, L0_ffn_router_b, L0_ffn_W1, L0_ffn_b1, L0_ffn_W2, L0_ffn_b2, L1_gnn_w1_s, L1_gnn_w1_v, L1_gnn_wsc_s, L1_gnn_wsc_v, L1_gnn_w2_s, L1_gnn_w2_v, L1_gnn_fc_w1, L1_gnn_fc_w2, L1_gnn_fc_w3, L1_gnn_g_s, L1_gnn_g_v, L1_ffn_router_w1, L1_ffn_router_b1, L1_ffn_router_w2, L1_ffn_router_b2, L1_ffn_expert_w1, L1_ffn_expert_b1, L1_ffn_expert_w2, L1_ffn_expert_b2, L1_ffn_expert_w3, L1_ffn_expert_b3, L2_gnn_Wq, L2_gnn_bq, L2_gnn_Wk, L2_gnn_bk, L2_gnn_Wv, L2_gnn_bv, L2_gnn_Wo, L2_gnn_bo, L2_gnn_W1, L2_gnn_b1, L2_gnn_W2, L2_gnn_b2, L2_gnn_g1, L2_gnn_be1, L2_gnn_g2, L2_gnn_be2, L2_ffn_Wr, L2_ffn_br, L2_ffn_W1, L2_ffn_b1, L2_ffn_g1, L2_ffn_be1, L2_ffn_m1, L2_ffn_v1, L2_ffn_W2, L2_ffn_b2, L2_ffn_g2, L2_ffn_be2, L2_ffn_m2, L2_ffn_v2, L2_ffn_Wo, L2_ffn_bo, L3_gnn_W, L3_gnn_att, L3_ffn_router_w, L3_ffn_w1, L3_ffn_b1, L3_ffn_w2, L3_ffn_b2):
    import jax
    import jax.numpy as jnp

    def _L0_gnn_ref(x, edge, W, a):
        import jax, jax.numpy as jnp
        import numpy as np
        N = 50000
        E_RAND = 25000
        F_IN = 256
        F_OUT = 256
        ALPHA = 0.2
        n = x.shape[0]
        f_out = W.shape[1]
        h = x @ W
        src, dst = (edge[0], edge[1])
        s = h @ a[:f_out]
        t = h @ a[f_out:]
        logit = s[src] + t[dst]
        e = jnp.exp(-jax.nn.leaky_relu(logit, ALPHA))
        rowsum = jax.ops.segment_sum(e, src, num_segments=n)
        msg = e[:, None] * h[dst]
        h_prime = jax.ops.segment_sum(msg, src, num_segments=n)
        h_prime = h_prime / rowsum[:, None]
        return jax.nn.relu(h_prime)

    def _L0_ffn_ref(x, router_w, router_b, W1, b1, W2, b2):
        import jax, jax.numpy as jnp
        import numpy as np
        B, K, D = (512, 16, 256)
        E = 32
        H = int(D * 0.25)
        xf = x.reshape(-1, D)
        logits = xf @ router_w.T + router_b
        idx = jnp.argmax(logits, axis=-1)
        w1t = jnp.take(W1, idx, axis=0)
        h = jnp.einsum('nd,ndh->nh', xf, w1t) + jnp.take(b1, idx, axis=0)
        h = jax.nn.relu(h)
        w2t = jnp.take(W2, idx, axis=0)
        out = jnp.einsum('nh,nhd->nd', h, w2t) + jnp.take(b2, idx, axis=0)
        out = jax.nn.relu(out)
        return out.reshape(x.shape)

    def _L1_gnn_ref(node_hiddens, edge_attr, edge_sh, w1_s, w1_v, wsc_s, wsc_v, w2_s, w2_v, fc_w1, fc_w2, fc_w3, g_s, g_v, edge_index):
        import jax, jax.numpy as jnp
        import numpy as np
        N_NODES = 625
        N_EDGES = 10000
        MUL = 64
        NUM_BASIS = 8
        INV_SQRT3 = 0.5773502691896258
        EPS = 1e-05
        N = node_hiddens.shape[0]
        xs = node_hiddens[:, :MUL]
        xv = node_hiddens[:, MUL:].reshape(N, MUL, 3)
        h = jax.nn.silu(edge_attr @ fc_w1 * (1.0 / np.sqrt(float(NUM_BASIS))))
        h = jax.nn.silu(h @ fc_w2 * (1.0 / np.sqrt(64.0)))
        w = h @ fc_w3 * (1.0 / np.sqrt(64.0))
        wA, wB, wC, wD = jnp.split(w, 4, axis=1)
        inv = 1.0 / np.sqrt(float(MUL))
        sc_s = xs @ wsc_s * inv
        sc_v = jnp.einsum('nud,uv->nvd', xv, wsc_v) * inv
        ys = xs @ w1_s * inv
        yv = jnp.einsum('nud,uv->nvd', xv, w1_v) * inv
        src = edge_index[0]
        dst = edge_index[1]
        es = ys[dst]
        ev = yv[dst]
        sh0 = edge_sh[:, :1]
        sh1 = edge_sh[:, 1:]
        m0a = wA * es * sh0
        m0b = wD * jnp.einsum('eud,ed->eu', ev, sh1) * INV_SQRT3
        m1a = wB[:, :, None] * es[:, :, None] * sh1[:, None, :]
        m1b = wC[:, :, None] * ev * sh0[:, :, None]
        mid_s = jnp.concatenate([m0a, m0b], axis=1)
        mid_v = jnp.concatenate([m1a, m1b], axis=1)
        ns = jax.ops.segment_sum(mid_s, src, num_segments=N)
        nv = jax.ops.segment_sum(mid_v, src, num_segments=N)
        deg = jax.ops.segment_sum(jnp.ones((src.shape[0],), node_hiddens.dtype), src, num_segments=N)
        dn = jax.lax.rsqrt(jnp.maximum(deg, 1.0))
        ns = ns * dn[:, None]
        nv = nv * dn[:, None, None]
        inv2 = 1.0 / np.sqrt(2.0 * MUL)
        os_ = ns @ w2_s * inv2 + sc_s
        ov = jnp.einsum('nud,uv->nvd', nv, w2_v) * inv2 + sc_v
        os_ = os_ * jax.lax.rsqrt(jnp.mean(os_ * os_, axis=1, keepdims=True) + EPS) * g_s
        rms_v = jax.lax.rsqrt(jnp.mean(ov * ov, axis=(1, 2))[:, None, None] + EPS)
        ov = ov * rms_v * g_v[None, :, None]
        return jnp.concatenate([os_, ov.reshape(N, 3 * MUL)], axis=1)

    def _L1_ffn_ref(features, router_w1, router_b1, router_w2, router_b2, expert_w1, expert_b1, expert_w2, expert_b2, expert_w3, expert_b3):
        import jax, jax.numpy as jnp
        import numpy as np
        E, D, H, TOP_K = (6, 256, 256, 2)
        ROUTER_H = D // 2
        rh = jax.nn.relu(features @ router_w1 + router_b1)
        expert_logits = jax.nn.softmax(rh @ router_w2 + router_b2, axis=-1)
        top_w, top_i = jax.lax.top_k(expert_logits, TOP_K)
        routing_weights = jax.nn.softmax(top_w, axis=-1)
        h1 = jax.nn.relu(jnp.einsum('bsd,edh->bseh', features, expert_w1) + expert_b1)
        h2 = jax.nn.relu(jnp.einsum('bseh,ehf->bsef', h1, expert_w2) + expert_b2)
        expert_out = jnp.einsum('bsef,efo->bseo', h2, expert_w3) + expert_b3
        sel = jnp.take_along_axis(expert_out, top_i[:, :, :, None], axis=2)
        combined = jnp.sum(sel * routing_weights[..., None], axis=2)
        return combined

    def _L2_gnn_ref(h, src, dst, Wq, bq, Wk, bk, Wv, bv, Wo, bo, W1, b1, W2, b2, g1, be1, g2, be2):
        import jax, jax.numpy as jnp
        import numpy as np
        N_NODES = 3125
        N_EDGES = 50000
        HID = 256
        HEADS = 4
        HEAD_DIM = HID // HEADS
        EPS = 1e-05

        def _layernorm(x, g, b):
            mu = jnp.mean(x, axis=-1, keepdims=True)
            var = jnp.mean(jnp.square(x - mu), axis=-1, keepdims=True)
            return (x - mu) * jax.lax.rsqrt(var + EPS) * g + b
        N = h.shape[0]
        scale = HEAD_DIM ** (-0.5)
        h_norm = _layernorm(h, g1, be1)
        Q = (h_norm @ Wq + bq).reshape(N, HEADS, HEAD_DIM)
        K = (h_norm @ Wk + bk).reshape(N, HEADS, HEAD_DIM)
        V = (h_norm @ Wv + bv).reshape(N, HEADS, HEAD_DIM)
        logits = jnp.einsum('ehd,ehd->eh', Q[dst], K[src]) * scale
        seg_max = jax.ops.segment_max(logits, dst, num_segments=N)
        e = jnp.exp(logits - seg_max[dst])
        seg_sum = jax.ops.segment_sum(e, dst, num_segments=N)
        w = e / seg_sum[dst]
        msg = V[src] * w[:, :, None]
        h_new = jax.ops.segment_sum(msg, dst, num_segments=N).reshape(N, HID)
        h_attn = h_new @ Wo + bo
        h = h + h_attn
        h2 = _layernorm(h, g2, be2)
        ffn = jax.nn.relu(h2 @ W1 + b1) @ W2 + b2
        return h + ffn

    def _L2_ffn_ref(x, Wr, br, W1, b1, g1, be1, m1, v1, W2, b2, g2, be2, m2, v2, Wo, bo):
        import jax, jax.numpy as jnp
        import numpy as np
        BN_EPS = 0.001

        def _bn(h, g, b, m, v):
            return g * (h - m) * jax.lax.rsqrt(v + BN_EPS) + b
        feat = jnp.mean(x, axis=0)
        w = jax.nn.softmax(feat @ Wr + br, axis=-1)
        h = jnp.einsum('bfd,edh->bfeh', x, W1) + b1
        h = jax.nn.relu(_bn(h, g1, be1, m1, v1))
        h = jnp.einsum('bfeh,ehk->bfek', h, W2) + b2
        h = jax.nn.relu(_bn(h, g2, be2, m2, v2))
        y = jnp.einsum('bfeh,ehd->bfed', h, Wo) + bo
        return jnp.einsum('bfed,fe->bfd', y, w)

    def _L3_gnn_ref(h, W, att, src, dst):
        import jax, jax.numpy as jnp
        import numpy as np
        NEG = -1000.0
        SLOPE = 0.01
        N_NODES, N_EDGES, D_IN, D_OUT, N_HEADS = (3125, 50000, 256, 64, 4)
        N = h.shape[0]
        H, _, F = W.shape
        z = jnp.einsum('nd,hdf->nhf', h, W)
        a_src, a_dst = (att[:, :F], att[:, F:])
        es = jnp.einsum('nhf,hf->nh', z, a_src)
        ed = jnp.einsum('nhf,hf->nh', z, a_dst)
        e = jax.nn.leaky_relu(es[src] + ed[dst], SLOPE)
        e = jnp.where(e == 0.0, NEG, e)
        m = jax.ops.segment_max(e, dst, num_segments=N)
        m = jnp.where(jnp.isfinite(m), m, 0.0)
        ex = jnp.exp(e - m[dst])
        denom = jax.ops.segment_sum(ex, dst, num_segments=N)
        safe = jnp.where(denom[dst] > 0.0, denom[dst], 1.0)
        alpha = ex / safe
        out = jax.ops.segment_sum(alpha[:, :, None] * z[src], dst, num_segments=N)
        return out.reshape(N, H * F)

    def _L3_ffn_ref(input_embeddings, router_w, w1, b1, w2, b2):
        import jax, jax.numpy as jnp
        import numpy as np
        NUM_EXPERTS = 8
        TOP_K = 2
        B, S, D = (8, 256, 256)

        def _moe(tokens, router_w, w1, b1, w2, b2):
            N = tokens.shape[0]
            E = router_w.shape[0]
            logits = tokens.astype(jnp.float32) @ router_w.astype(jnp.float32).T
            probs = jax.nn.softmax(logits, axis=-1)
            rw, re = jax.lax.top_k(probs, TOP_K)
            if TOP_K > 1:
                rw = rw / jnp.maximum(rw.sum(-1, keepdims=True), 1e-12)
            rw = rw.astype(tokens.dtype)
            combine = jnp.zeros((N, E), tokens.dtype).at[jnp.arange(N)[:, None], re].set(rw)
            out = tokens
            for e in range(E):
                h = jax.nn.gelu(tokens @ w1[e] + b1[e], approximate=False)
                y = h @ w2[e] + b2[e]
                out = out + combine[:, e:e + 1] * y
            return out
        b, s, d = input_embeddings.shape
        tokens = input_embeddings.reshape(b * s, d)
        return _moe(tokens, router_w, w1, b1, w2, b2).reshape(b, s, d)
    edge_index = jnp.stack([src, dst])
    x = x + _L0_gnn_ref(_layernorm(x, axis=-1), edge_index, L0_gnn_W, L0_gnn_a)
    x = x + _L0_ffn_ref(_layernorm(x, axis=-1)[None], L0_ffn_router_w, L0_ffn_router_b, L0_ffn_W1, L0_ffn_b1, L0_ffn_W2, L0_ffn_b2)[0]
    x = x + _L1_gnn_ref(_layernorm(x, axis=-1), edge_attr_8, edge_attr_4, L1_gnn_w1_s, L1_gnn_w1_v, L1_gnn_wsc_s, L1_gnn_wsc_v, L1_gnn_w2_s, L1_gnn_w2_v, L1_gnn_fc_w1, L1_gnn_fc_w2, L1_gnn_fc_w3, L1_gnn_g_s, L1_gnn_g_v, edge_index)
    x = x + _L1_ffn_ref(_layernorm(x, axis=-1)[None], L1_ffn_router_w1, L1_ffn_router_b1, L1_ffn_router_w2, L1_ffn_router_b2, L1_ffn_expert_w1, L1_ffn_expert_b1, L1_ffn_expert_w2, L1_ffn_expert_b2, L1_ffn_expert_w3, L1_ffn_expert_b3)[0]
    x = x + _L2_gnn_ref(_layernorm(x, axis=-1), src, dst, L2_gnn_Wq, L2_gnn_bq, L2_gnn_Wk, L2_gnn_bk, L2_gnn_Wv, L2_gnn_bv, L2_gnn_Wo, L2_gnn_bo, L2_gnn_W1, L2_gnn_b1, L2_gnn_W2, L2_gnn_b2, L2_gnn_g1, L2_gnn_be1, L2_gnn_g2, L2_gnn_be2)
    x = x + _L2_ffn_ref(_layernorm(x, axis=-1)[None], L2_ffn_Wr, L2_ffn_br, L2_ffn_W1, L2_ffn_b1, L2_ffn_g1, L2_ffn_be1, L2_ffn_m1, L2_ffn_v1, L2_ffn_W2, L2_ffn_b2, L2_ffn_g2, L2_ffn_be2, L2_ffn_m2, L2_ffn_v2, L2_ffn_Wo, L2_ffn_bo)[0]
    x = x + _L3_gnn_ref(_layernorm(x, axis=-1), L3_gnn_W, L3_gnn_att, src, dst)
    x = x + _L3_ffn_ref(_layernorm(x, axis=-1)[None], L3_ffn_router_w, L3_ffn_w1, L3_ffn_b1, L3_ffn_w2, L3_ffn_b2)[0]
    return x

_drawn_inputs = setup_inputs


def setup_inputs(seed=0):
    import zlib

    import numpy as np

    out = dict(_drawn_inputs(seed))
    spreads = {'L1_gnn_g_s': (1.0, 0.2),
     'L1_gnn_g_v': (1.0, 0.2),
     'L1_ffn_router_b1': (0.0, 0.1),
     'L1_ffn_router_b2': (0.0, 0.1),
     'L1_ffn_expert_b1': (0.0, 0.614),
     'L1_ffn_expert_b2': (0.0, 0.335),
     'L1_ffn_expert_b3': (0.0, 0.1),
     'L2_gnn_bq': (0.0, 0.613),
     'L2_gnn_bk': (0.0, 2.0),
     'L2_gnn_bv': (0.0, 0.1),
     'L2_gnn_bo': (0.0, 0.1),
     'L2_gnn_b1': (0.0, 0.1),
     'L2_gnn_b2': (0.0, 0.1),
     'L2_gnn_g1': (1.0, 0.2),
     'L2_gnn_be1': (0.0, 0.1),
     'L2_gnn_g2': (1.0, 0.2),
     'L2_gnn_be2': (0.0, 0.268),
     'L2_ffn_br': (0.0, 0.662),
     'L2_ffn_b1': (0.0, 0.53),
     'L2_ffn_g1': (1.0, 0.6),
     'L2_ffn_be1': (0.0, 0.514),
     'L2_ffn_m1': (0.0, 0.502),
     'L2_ffn_v1': (1.0, 0.6),
     'L2_ffn_b2': (0.0, 0.409),
     'L2_ffn_g2': (1.0, 0.565),
     'L2_ffn_be2': (0.0, 0.451),
     'L2_ffn_m2': (0.0, 0.397),
     'L2_ffn_v2': (1.0, 0.6),
     'L2_ffn_bo': (0.0, 0.323),
     'L3_ffn_b1': (0.0, 0.577),
     'L3_ffn_b2': (0.0, 0.397)}
    factors = {'L0_ffn_b1': 3.785}
    for name, (base, spread) in spreads.items():
        noise = np.random.default_rng([zlib.crc32(name.encode()), seed]).standard_normal(out[name].shape)
        drawn = base * np.exp(spread * noise) if base else spread * noise
        out[name] = jnp.asarray(drawn.astype(out[name].dtype))
    for name, factor in factors.items():
        out[name] = (out[name] * factor).astype(out[name].dtype)
    return out
```

```python
import concourse.bass as bass
from concourse import mybir
from contextlib import ExitStack

FP = mybir.dt.float32
BF = mybir.dt.bfloat16
I32 = mybir.dt.int32
U32 = mybir.dt.uint32
ALU = mybir.AluOpType
ACT = mybir.ActivationFunctionType
AX = mybir.AxisListType

NN = 3125
NE = 50000
D = 256
NT = 25
NP_ = NT * 128
EC = 391
NC = 416
G = 4
NSLOT = 58
NOBODY = -1.0e30
NG = NC // G
TAIL = NN - (NT - 1) * 128


class Queue:

    def __init__(self, sem):
        self.sem = sem
        self.n = 0
        self.todo = []
        self.passed = {}

    def wait(self, *marks):
        for sem, value in marks:
            if self.passed.get(id(sem), 0) < value:
                self.passed[id(sem)] = value
                self.todo.append(lambda e, s=sem, v=value: e.wait_ge(s, v))

    def do(self, fn, *marks):
        self.wait(*marks)
        self.n += 1
        self.todo.append(lambda e: fn(e).then_inc(self.sem, 1))
        return (self.sem, self.n)

    def raw(self, fn, *marks):
        self.wait(*marks)
        self.todo.append(fn)

    def dma(self, fn, sem, *marks):
        self.wait(*marks)
        self.todo.append(lambda e: fn(e).then_inc(sem.sem, 16))
        return sem.more()

    def last(self):
        return (self.sem, self.n)

    def run(self, e):
        for fn in self.todo:
            fn(e)


class DSem:
    def __init__(self, sem):
        self.sem = sem
        self.n = 0

    def more(self):
        self.n += 16
        return (self.sem, self.n)

    def all(self):
        return (self.sem, self.n)


def build(nc, A, out, stop=8):
    ctx = ExitStack()
    with ctx:

        def sb(name, shape, dt=FP):
            return ctx.enter_context(nc.sbuf_tensor(name, shape, dt))

        def dsem(name):
            return DSem(ctx.enter_context(nc.semaphore(name)))

        def dram(name, shape, dt=FP):
            return nc.dram_tensor(name, shape, dt).ap()

        pe, dve, act, pool, sp = [Queue(ctx.enter_context(nc.semaphore(f"q_{n}")))
                                  for n in ("pe", "dve", "act", "pool", "sp")]
        compute = (pe, dve, act, pool)
        dsems = []

        def ring(name, n):
            r = [dsem(f"{name}{i}") for i in range(n)]
            dsems.extend(r)
            return r

        def barrier():
            marks = [q.last() for q in compute] + [d.all() for d in dsems]
            for q in (pe, dve, act, pool, sp):
                q.wait(*[m for m in marks if m[1]])

        X = sb("X", [128, NT, D])
        XNT = sb("XNT", [128, 2, NP_])
        ident = sb("ident", [128, 128])
        iota = sb("iota", [128, 128])
        iotab = sb("iotab", [128, 128], BF)
        identb = sb("identb", [128, 128], BF)
        onesb = sb("onesb", [128, 1], BF)
        iotai = sb("iotai", [128, 128], I32)
        iotac = sb("iotac", [128, NC])
        ones = sb("ones", [128, 128])
        tri = sb("tri", [128, 128])
        padf = sb("padf", [128, 1])
        real = sb("real", [128, 1])
        stats = sb("stats", [128, NT, 6])
        mv = sb("mv", [128, NT, 2])
        eps = sb("eps", [128, 2])
        rstd = sb("rstd", [128, NT])
        RSE = sb("RSE", [128, 64], I32)
        TTR = sb("TTR", [1, 64], I32)
        TTS = sb("TTS", [1, NC], I32)
        TTD = sb("TTD", [1, NC], I32)
        BIG = 36900
        bigt = sb("bigt", [128, BIG])
        cur = [0]
        most = [0]

        def region(shape, dt=FP):
            n = 1
            for s in shape[1:]:
                n *= s
            if dt == BF:
                n = (n + 1) // 2
            a = bigt[0:shape[0], cur[0]:cur[0] + n]
            cur[0] += n
            assert cur[0] <= BIG, cur[0]
            most[0] = max(most[0], cur[0])
            if dt != FP:
                a = a.bitcast(dt)
            if len(shape) == 3:
                a = a.rearrange("p (a b) -> p a b", a=shape[1])
            elif len(shape) == 4:
                a = a.rearrange("p (a b c) -> p a b c", a=shape[1], b=shape[2])
            elif len(shape) == 5:
                a = a.rearrange("p (a b c d) -> p a b c d", a=shape[1], b=shape[2], c=shape[3])
            return a

        PB = [ctx.enter_context(nc.psum_tensor(f"PB{i}", [128, 512], FP)) for i in range(8)]

        s_w = ring("s_w", 2)
        s_x = ring("s_x", 1)
        s_tab = ring("s_tab", 4)
        s_g = ring("s_g", 4)
        s_h = ring("s_h", 4)
        s_in = ring("s_in", 4)
        s_g8 = ring("s_gg", 8)
        s_r = ring("s_r", 12)
        s_sc = ring("s_sc", 1)
        s_fill = ring("s_fill", 1)

        RECS = dram("RECS", [NC * 128, 16])
        RECD = dram("RECD", [NC * 128, 2])
        HTAB = dram("HTAB", [NP_, 258])
        YTAB = dram("YTAB", [NP_, 256])
        KTAB = dram("KTAB", [NP_, 256])
        VTAB = dram("VTAB", [NP_, 260])
        ETAB = dram("ETAB", [NP_, 4])
        SRT = dram("SRT", [NSLOT * 128, 256])
        OUTS = dram("OUTS", [NSLOT * 128, 256])

        pool.do(lambda e: e.memset(ident[:, :], 0.0))
        m = pool.do(lambda e: e.memset(tri[:, :], 1.0))
        m_id = pool.do(lambda e: e.affine_select(out=ident[:, :], in_=ident[:, :], compare_op=ALU.not_equal, fill=1.0,
                                          base=0, pattern=[[-1, 128]], channel_multiplier=1), m)
        m_tri = pool.do(lambda e: e.affine_select(out=tri[:, :], in_=tri[:, :], compare_op=ALU.is_gt, fill=0.0,
                                          base=0, pattern=[[1, 128]], channel_multiplier=-1), m)
        m_iota = pool.do(lambda e: e.iota(iotai[:, :], pattern=[[1, 128]], base=0, channel_multiplier=0))
        ici = region([128, NC], I32)
        m_ic = pool.do(lambda e: e.iota(ici, pattern=[[1, NC]], base=0, channel_multiplier=0))
        dve.do(lambda e: e.tensor_copy(iota[:, :], iotai[:, :]), m_iota)
        dve.do(lambda e: e.tensor_copy(iotac[:, :], ici), m_ic)
        m_1 = dve.do(lambda e: e.memset(ones[:, :], 1.0))
        zf = region([128, NSLOT * 128])
        mzf = dve.do(lambda e: e.memset(zf, 0.0))
        for h in range(2):
            sp.dma(lambda e, h=h: e.dma_start(
                SRT[h * NSLOT * 64:(h + 1) * NSLOT * 64, :].rearrange("(p j) d -> p (j d)", p=128), zf), s_fill[0], mzf)
        dve.do(lambda e: e.tensor_copy(iotab[:, :], iotai[:, :]))
        dve.do(lambda e: e.tensor_copy(identb[:, :], ident[:, :]), m_id)
        dve.do(lambda e: e.memset(onesb[:, :], 1.0))
        m = dve.do(lambda e: e.memset(eps[:, 0:1], 1e-5))
        dve.do(lambda e: e.memset(eps[:, 1:2], 1e-3), m)
        pool.do(lambda e: e.memset(padf[:, :], 1.0))
        pool.do(lambda e: e.affine_select(out=padf[:, :], in_=padf[:, :], compare_op=ALU.is_ge, fill=0.0,
                                          base=-TAIL, pattern=[[0, 1]], channel_multiplier=1), pool.last())
        dve.do(lambda e: e.tensor_scalar(real[:, :], padf[:, :], -1.0, 1.0, ALU.mult, ALU.add), pool.last())
        m0 = dve.do(lambda e: e.memset(X[:, NT - 1, :], 0.0))
        xm = A["x"]
        for h in range(4):
            sp.dma(lambda e, h=h: e.dma_start(X[:, 6 * h:6 * h + 6, :],
                                         xm[768 * h:768 * h + 768, :].rearrange("(t p) d -> p t d", p=128)), s_x[0])
        sp.dma(lambda e: e.dma_start(X[0:TAIL, NT - 1, :], xm[(NT - 1) * 128:NN, :]), s_x[0], m0)
        barrier()
        cur[0] = 0

        def got(mk, *key):
            return [mk[key]] if key in mk else []

        def pipeline(n, stages):
            deep = max(lag for lag, _ in stages)
            for i in range(n + deep):
                for lag, step in stages:
                    if 0 <= i - lag < n:
                        step(i - lag)

        def rank(T, n, E, tt, ntt, mT, ci):
            oh = region([128, E, n])
            sc = region([128, E, n])
            cnt = region([128, E])
            off = region([128, E])
            tot = region([128, E])
            toti = region([128, E], I32)
            nch = region([128, E])
            cum = region([128, E])
            B = region([128, E])
            ta = region([128, ntt])
            W = region([128, n])
            pos = region([128, n], I32)
            ek = region([128, E])
            m = dve.do(lambda e: e.tensor_copy(ek, iota[:, 0:E]))
            m1 = dve.do(lambda e: e.tensor_tensor(oh, T.unsqueeze(1).to_broadcast([128, E, n]),
                                                  ek.unsqueeze(2).to_broadcast([128, E, n]), ALU.is_equal), mT, m)
            ohf, scf = oh.rearrange("p a b -> p (a b)"), sc.rearrange("p a b -> p (a b)")
            one = ones[:, 0:1].to_broadcast([128, E * n])
            m2 = dve.do(lambda e: e.tensor_tensor_scan(out=scf, data0=one, data1=ohf, initial=0.0,
                                                       op0=ALU.mult, op1=ALU.add), m1)
            m = dve.do(lambda e: e.tensor_copy(cum, sc[:, :, n - 1]), m2)
            m3 = dve.do(lambda e: e.tensor_copy(cnt, cum), m)
            m3 = dve.do(lambda e: e.tensor_tensor(cnt[:, 1:E], cum[:, 1:E], cum[:, 0:E - 1], ALU.subtract), m3)
            mB = dve.do(lambda e: e.tensor_tensor(B, cnt, cum, ALU.subtract), m3)
            pe.do(lambda e: e.matmul(PB[0][:, 0:E], tri[:, :], cnt, start=True, stop=True), m3)
            mp = pe.do(lambda e: e.matmul(PB[1][:, 0:E], ones[:, :], cnt, start=True, stop=True))
            mB = dve.do(lambda e: e.tensor_tensor(B, B, PB[0][:, 0:E], ALU.add), mp, mB)
            m = dve.do(lambda e: e.tensor_scalar(tot, PB[1][:, 0:E], 127.0, None, ALU.add), mp)
            m = dve.do(lambda e: e.tensor_copy(toti, tot), m)
            m = dve.do(lambda e: e.tensor_scalar(toti, toti, 7, None, ALU.arith_shift_right), m)
            m = dve.do(lambda e: e.tensor_copy(nch, toti), m)
            m = dve.do(lambda e: e.tensor_tensor_scan(out=cum, data0=ones[:, 0:E], data1=nch, initial=0.0,
                                                      op0=ALU.mult, op1=ALU.add), m)
            mc = dve.do(lambda e: e.tensor_tensor(nch, cum, nch, ALU.subtract), m)
            m = dve.do(lambda e: e.tensor_scalar(tot, nch, 128.0, -1.0, ALU.mult, ALU.add), mc)
            m = dve.do(lambda e: e.tensor_tensor(B, B, tot, ALU.add), m, mB)
            m = dve.do(lambda e: e.tensor_tensor(sc, sc, B.unsqueeze(2).to_broadcast([128, E, n]), ALU.add), m)
            m = dve.do(lambda e: e.tensor_tensor(sc, sc, oh, ALU.mult), m)
            m = dve.do(lambda e: e.tensor_reduce(W, sc.rearrange("p a b -> p b a"), axis=AX.X, op=ALU.add), m)
            m_pos = dve.do(lambda e: e.tensor_copy(pos, W), m)
            ge = oh.rearrange("p a b -> p (a b)")[:, 0:min(E * n, E * ntt)]
            m = dve.do(lambda e: e.memset(ta, 0.0), m_pos)
            for t in range(1, E):
                m = dve.do(lambda e, t=t: e.scalar_tensor_tensor(out=ta, in0=iotac[:, 0:ntt], scalar=nch[:, t:t + 1],
                                                                 in1=ta, op0=ALU.is_ge, op1=ALU.add), m)
            m_tt = dve.do(lambda e: e.tensor_copy(tt[0:1, 0:ntt], ta[0:1, :]), m)
            return pos, m_pos, m_tt

        def sort(key, other, width, rec_dram, tt, attrs):
            cur[0] = 0
            K = region([128, EC], I32)
            O = region([128, EC], I32)
            ti = region([128, EC], I32)
            T = region([128, EC])
            rec = region([128, EC, width])
            fill = region([128, 104, width])
            raw = region([128, EC, 8]) if attrs else None
            last = NE - 127 * EC
            dve.do(lambda e: e.memset(K, 4096))
            mz = dve.do(lambda e: e.memset(O, 0))
            if attrs:
                mz = dve.do(lambda e: e.memset(raw, 0.0))
                mz = dve.do(lambda e: e.memset(rec, 0.0))
            mf = dve.do(lambda e: e.memset(fill, 0.0))
            mf = dve.do(lambda e: e.memset(fill[:, :, 0:1], -1.0), mf)
            mf = dve.do(lambda e: e.memset(fill.bitcast(I32)[:, :, 1:2], NP_ - 1), mf)

            def load(dst, src, w):
                full = src[0:127 * EC].rearrange("(p c) -> p c", p=127) if w == 1 else \
                    src[0:127 * EC, :].rearrange("(p c) f -> p (c f)", p=127)
                tail = src[127 * EC:NE].rearrange("(p c) -> p c", p=1) if w == 1 else \
                    src[127 * EC:NE, :].rearrange("(p c) f -> p (c f)", p=1)
                sp.dma(lambda e: e.dma_start(dst[0:127, :], full), s_w[0], mz)
                return sp.dma(lambda e: e.dma_start(dst[127:128, 0:last * w], tail), s_w[0], mz)
            load(K, key, 1)
            ml = load(O, other, 1)
            ma = []
            if attrs:
                r4 = raw.rearrange("p c f -> p (c f)")[:, 0:EC * 4]
                ml = load(r4, attrs[0], 4)
                m4 = act.do(lambda e: e.activation(rec[:, :, 2:6], r4.rearrange("p (c f) -> p c f", f=4), ACT.Copy), ml)
                sp.wait(m4)
                r8 = raw.rearrange("p c f -> p (c f)")
                m8 = load(r8, attrs[1], 8)
                ma = [act.do(lambda e: e.activation(rec[:, :, 6:14], raw, ACT.Copy), m8)]
            for h in range(4):
                m_fill = sp.dma(lambda e, h=h: e.dma_start(
                    rec_dram[h * 104 * 128:(h + 1) * 104 * 128, :].rearrange("(p j) f -> p j f", p=128), fill), s_fill[0], mf)
            mt = dve.do(lambda e: e.tensor_scalar(ti, K, 7, None, ALU.arith_shift_right), ml)
            mT = dve.do(lambda e: e.tensor_copy(T, ti), mt)
            mt = dve.do(lambda e: e.tensor_scalar(ti, K, 127, None, ALU.bitwise_and), mT)
            mk = dve.do(lambda e: e.tensor_copy(rec[:, :, 0:1], ti.unsqueeze(2)), mt)
            mr = dve.do(lambda e: e.tensor_copy(rec.bitcast(I32)[:, :, 1:2], O.unsqueeze(2)), mk)
            pos, m_pos, m_tt = rank(T, EC, NT, tt, NC, mT, None)
            pool.wait(m_fill, m_pos, mr, *ma)
            for c in range(EC):
                n = 128 if c < last else 127
                pool.dma(lambda e, c=c, n=n: e.indirect_dma_start(
                    out=rec_dram, out_offset=bass.IndirectOffsetOnAxis(ap=pos[0:n, c:c + 1].bitcast(U32), axis=0),
                    in_=rec[0:n, c, :], in_offset=None), s_sc[0])
            barrier()
            cur[0] = 0

        def inv_sqrt(dst, src, m, eps_col=0, scale=1.0):
            m = act.do(lambda e: e.activation(dst, src, ACT.Sqrt, bias=eps[:, eps_col:eps_col + 1], scale=scale), m)
            return dve.do(lambda e: e.reciprocal(dst, dst), m)

        def ln_stats(src, *m):
            ms = [dve.do(lambda e, t=t: e.bn_stats(out=stats[:, t, :], in_=src[:, t, :]), *m) for t in range(NT)]
            for t in range(NT):
                m = dve.do(lambda e, t=t: e.bn_aggr(out=mv[:, t, :], in_=stats[:, t, :]), ms[t])
            return inv_sqrt(rstd[:, :], mv[:, :, 1], m)

        def plain_ln(src, dst):
            def produce(t, b, deps):
                return dve.do(lambda e: e.tensor_scalar(dst[:, b, :], src[:, t, :], mv[:, t, 0:1], rstd[:, t:t + 1],
                                                        ALU.subtract, ALU.mult), *deps)
            return produce

        def copy_evac(t, bank, m):
            return act.do(lambda e: e.activation(XNT[:, :, t * 128:(t + 1) * 128],
                                                 bank[:, 0:256].rearrange("p (k n) -> p k n", k=2), ACT.Copy), m)

        def affine_evac(gc, bc):
            def evac(t, bank, m):
                for k in range(2):
                    r = act.do(lambda e, k=k: e.activation(XNT[:, k, t * 128:(t + 1) * 128],
                                                           bank[:, k * 128:(k + 1) * 128], ACT.Identity,
                                                           bias=bc[:, k:k + 1], scale=gc[:, k:k + 1]), m)
                return r
            return evac

        def transpose_tiles(produce, xn, nb, m, evac=copy_evac):
            tr_at, ev_at = {}, {}
            for t in range(NT):
                b, p = t % nb, t % 2
                m1 = produce(t, b, [m] + ([tr_at[t - nb]] if t >= nb else []))

                def tr(e, b=b, p=p):
                    e.transpose(PB[p][:, 0:128], xn[:, b, 0:128], ident[:, :])
                    return e.transpose(PB[p][:, 128:256], xn[:, b, 128:256], ident[:, :])
                tr_at[t] = pe.do(tr, m1, *([ev_at[t - 2]] if t >= 2 else []))
                ev_at[t] = evac(t, PB[p], tr_at[t])
            return ev_at

        regs = {}

        def tiles_of(q, name, tt, first, count, store, slot, keys=NT):
            def fn(e):
                if name not in regs:
                    regs[name] = [e.alloc_register(f"{name}_{i}") for i in range(2 * G)]
                r = regs[name][(slot % 2) * G:(slot % 2) * G + count]
                if count == 1:
                    e.load(r[0], tt[0:1, first:first + 1])
                else:
                    e.load(r, tt[0:1, first:first + count])
                for j in range(count):
                    store[first + j] = e.snap(r[j], min_val=0, max_val=keys - 1)
            q.raw(fn)

        def keys_of(rec):
            return rec[:, :, 0]

        def onehots(mk, key, OH, nb, io):
            def step(g):
                for j in range(G):
                    mk["oh", g] = dve.do(lambda e, j=j: e.tensor_scalar(
                        OH[:, g % nb, j, :], io, key(g, j), None, ALU.is_equal), *got(mk, "oh_free", g - nb))
            return step

        def turn_onehots(mk, OH, nb, OHT, nbt):
            def banks(g):
                return PB[g % 2][:, :] if OH.dtype == FP else PB[g % 2][:, 0:256].bitcast(BF)

            def tr(g):
                def fn(e):
                    for j in range(G):
                        r = e.transpose(banks(g)[:, j * 128:(j + 1) * 128], OH[:, g % nb, j, :],
                                        ident[:, :] if OH.dtype == FP else identb[:, :])
                    return r
                mk["oht_tr", g] = pe.do(fn, mk["oh", g], *got(mk, "oht", g - 2))

            def ev(g):
                mk["oht", g] = act.do(lambda e: e.activation(OHT[:, g % nbt, :], banks(g), ACT.Copy),
                                      mk["oht_tr", g], *got(mk, "oht_free", g - nbt))
            return tr, ev

        def split3(dst, src, tmp, *m):
            m = dve.do(lambda e: e.tensor_copy(dst[0], src), *m)
            m = dve.do(lambda e: e.tensor_tensor(tmp, src, dst[0], ALU.subtract), m)
            m = dve.do(lambda e: e.tensor_copy(dst[1], tmp), m)
            m = dve.do(lambda e: e.tensor_tensor(tmp, tmp, dst[1], ALU.subtract), m)
            return dve.do(lambda e: e.tensor_copy(dst[2], tmp), m)

        def gathers(mk, REC, dst, nb, table, sems, tag):
            def step(g):
                for j in range(G):
                    mk[tag, g] = pool.dma(lambda e, j=j: e.indirect_dma_start(
                        out=dst[:, g % nb, j, :], out_offset=None, in_=table,
                        in_offset=bass.IndirectOffsetOnAxis(ap=REC[:, g * G + j, 1:2].bitcast(U32), axis=0)),
                        sems[g % nb], *got(mk, tag + "_free", g - nb))
            return step

        def load2(dst, src, sem=0):
            return sp.dma(lambda e: e.dma_start(dst, src.rearrange("(k p) n -> p k n", p=128)), s_w[sem])

        def load1(dst, src):
            return sp.dma(lambda e: e.dma_start(dst, src), s_w[0])

        def load_rows(dst, src):
            return sp.dma(lambda e: e.dma_start(dst, src.partition_broadcast(128)), s_w[0])

        def l0_gnn():
            Wx = region([128, 2, 258])
            WT = region([128, 2, D])
            av = region([128, 2, 2])
            xn = region([128, 4, D])
            hb = region([128, 4, 258])
            S = region([128, NT])
            S3 = region([128, 3, 64], BF)
            ACC = region([128, NT, 258])
            REC = region([128, NC, 16])
            GB, OB, TB, EB = 7, 11, 4, 4
            Gt = region([128, GB, G, 258])
            OH = region([128, OB, G, 128], BF)
            OHe = region([128, 2, G, 128])
            OHT = region([128, TB, G * 128], BF)
            lg = region([128, EB, G])
            lr = region([128, EB, G])
            ev = region([128, EB, G])
            rs = region([128, NT])
            load2(Wx[:, :, 0:256], A["L0_gnn_W"])
            load2(WT, A["L0_gnn_WT"])
            m_w = load2(av, A["L0_gnn_a2"])
            m_rec = sp.dma(lambda e: e.dma_start(REC, RECS.rearrange("(c p) f -> p c f", p=128)), s_x[0])

            def wa(e):
                for k in range(2):
                    for o in range(2):
                        r = e.matmul(PB[7][:, 2 * k:2 * k + 2], WT[:, o, k * 128:(k + 1) * 128], av[:, o, :],
                                     start=(o == 0), stop=(o == 1))
                return r
            m = pe.do(wa, m_w)
            m_wx = dve.do(lambda e: e.tensor_copy(Wx[:, :, 256:258], PB[7][:, 0:4].rearrange("p (k c) -> p k c", k=2)), m)
            mz = dve.do(lambda e: e.memset(ACC, 0.0))
            m_one = dve.do(lambda e: e.memset(hb[:, :, 256:257], 1.0))
            m_xnt = transpose_tiles(plain_ln(X, xn), xn, 4, ln_stats(X))
            ev2 = {}
            for t in range(NT):
                p, b = 2 + t % 2, t % 4

                def mm(e, t=t, p=p):
                    for k in range(2):
                        r = e.matmul(PB[p][:, 0:258], XNT[:, k, t * 128:(t + 1) * 128], Wx[:, k, :],
                                     start=(k == 0), stop=(k == 1))
                    return r
                m1 = pe.do(mm, m_xnt[t], m_wx, *ev2.get(t - 2, []))
                free = [s_tab[b].all()] if s_tab[b].n else []
                m2 = act.do(lambda e, p=p, b=b: e.activation(hb[:, b, 0:256], PB[p][:, 0:256], ACT.Copy), m1, *free)
                dve.do(lambda e, p=p, b=b: e.tensor_copy(hb[:, b, 257:258], PB[p][:, 256:257]), m1, m2)
                m3 = dve.do(lambda e, p=p, t=t: e.tensor_copy(S[:, t:t + 1], PB[p][:, 257:258]))
                ev2[t] = [m2, m3]
                sp.dma(lambda e, t=t, b=b: e.dma_start(HTAB[t * 128:(t + 1) * 128, :], hb[:, b, :]), s_tab[b], m2, m3)
            pool.wait(*[d.all() for d in s_tab], m_rec)
            dve.wait(m_rec)
            m_S = split3([S3[:, k, 0:NT] for k in range(3)], S, rs, m3)
            pe.wait(m_S)
            mk, tp, tv = {("acc",): mz}, {}, {}

            def key_logits(g):
                tiles_of(pe, "pe", TTS, g * G, G, tp, g)

                def sg(e):
                    for j in range(G):
                        for k in range(3):
                            r = e.matmul(PB[2 + g % 2][:, j:j + 1], OHT[:, g % TB, j * 128:(j + 1) * 128],
                                         S3[:, k, bass.ds(tp[g * G + j], 1)], start=(k == 0), stop=(k == 2))
                    return r
                mk["oht_free", g] = mk["sg", g] = pe.do(sg, mk["oht", g], *got(mk, "lg", g - 2))

            def logits(g):
                mk["lg", g] = dve.do(lambda e: e.tensor_tensor(lg[:, g % EB, :], PB[2 + g % 2][:, 0:G],
                                                               Gt[:, g % GB, :, 257], ALU.add), mk["sg", g], mk["g", g])

            def leak(g):
                mk["lr", g] = dve.do(lambda e: e.scalar_tensor_tensor(
                    out=lr[:, g % EB, :], in0=lg[:, g % EB, :], scalar=0.2, in1=lg[:, g % EB, :],
                    op0=ALU.mult, op1=ALU.max), mk["lg", g])

            def expo(g):
                mk["e", g] = act.do(lambda e: e.activation(ev[:, g % EB, :], lr[:, g % EB, :], ACT.Exp, scale=-1.0),
                                    mk["lr", g])

            def weigh(g):
                for j in range(G):
                    mk["ohe", g] = dve.do(lambda e, j=j: e.tensor_scalar(
                        OHe[:, g % 2, j, :], OH[:, g % OB, j, :], ev[:, g % EB, j:j + 1], None, ALU.mult),
                        mk["e", g], *got(mk, "sum", g - 2))

            def total(g):
                for j in range(G):
                    bank = PB[4 + j]

                    def mm(e, j=j, bank=bank):
                        e.matmul(bank[:, 0:257], OHe[:, g % 2, j, :], Gt[:, g % GB, j, 0:257], start=True, stop=False)
                        return e.matmul(bank[:, 257:258], OH[:, g % OB, j, :], onesb[:, :], start=False, stop=True)
                    mk["sum", g, j] = pe.do(mm, mk["ohe", g], *got(mk, "added", g - 1, j))
                mk["sum", g] = mk["oh_free", g] = mk["g_free", g] = mk["sum", g, G - 1]

            def add(g):
                tiles_of(dve, "dve", TTS, g * G, G, tv, g)
                for j in range(G):
                    mk["acc",] = mk["added", g, j] = dve.do(lambda e, j=j: e.tensor_tensor(
                        ACC[:, bass.ds(tv[g * G + j], 1), :], ACC[:, bass.ds(tv[g * G + j], 1), :],
                        PB[4 + j][:, 0:258].unsqueeze(1), ALU.add), mk["sum", g, j], mk["acc",])
            tr, ev_ = turn_onehots(mk, OH, OB, OHT, TB)
            pipeline(NG, [(10, add), (9, total), (8, weigh), (7, expo), (6, leak), (5, logits), (4, key_logits),
                          (3, ev_), (2, tr), (1, onehots(mk, lambda g, j: REC[:, g * G + j, 0:1], OH, OB, iotab[:, :])),
                          (2, gathers(mk, REC, Gt, GB, HTAB, s_g8, "g"))])
            m = mk["acc",]
            dve.do(lambda e: e.tensor_copy(DEG[:, :], ACC[:, :, 257]), m)
            m = dve.do(lambda e: e.tensor_copy(rs, ACC[:, :, 256]), mk["acc",])
            m = dve.do(lambda e: e.tensor_tensor(rs[:, NT - 1:NT], rs[:, NT - 1:NT], padf[:, :], ALU.add), m)
            m = dve.do(lambda e: e.reciprocal(rs, rs), m)
            for t in range(NT):
                m1 = act.do(lambda e, t=t: e.activation(ACC[:, t, 0:256], ACC[:, t, 0:256], ACT.Relu,
                                                        scale=rs[:, t:t + 1]), m)
                dve.do(lambda e, t=t: e.tensor_tensor(X[:, t, :], X[:, t, :], ACC[:, t, 0:256], ALU.add), m1)

        def routed(name, E, K, NS, dims, W, B, func, router, choose, last_relu, keep=False):
            EP = max(E, 8)
            xs = region([128, NT, D])
            lgt = region([128, NT, EP])
            top = region([128, NT, 8])
            ix = region([128, NT, 8], U32)
            T = region([128, K * NT])
            rw = region([128, 2, NT])
            nl = len(W)
            Ws, Bs = [], []
            for l in range(nl):
                di, do = dims[l], dims[l + 1]
                kc = max(1, di // 128)
                w = region([min(di, 128), kc, E * do])
                b = region([128, E * do])
                for k in range(kc):
                    p = min(di, 128)
                    sp.dma(lambda e, w=w, k=k, p=p, l=l: e.dma_start(
                        w[:, k, :].rearrange("p (e n) -> p e n", e=E),
                        W[l][:, k * p:(k + 1) * p, :].rearrange("e p n -> p e n")), s_w[1])
                m_W = sp.dma(lambda e, b=b, l=l: e.dma_start(
                    b, B[l].rearrange("e n -> (e n)").partition_broadcast(128)), s_w[1])
                Ws.append(w)
                Bs.append(b)
            mz = dve.do(lambda e: e.memset(lgt, NOBODY))
            m_xnt = transpose_tiles(plain_ln(X, xs), xs, NT, ln_stats(X))
            m = router(lgt, m_xnt, mz)
            m = choose(lgt, top, ix, rw, m)
            for k in range(K):
                m = dve.do(lambda e, k=k: e.tensor_copy(T[:, k * NT:(k + 1) * NT], ix[:, :, k]), m)
            pos, m_pos, m_tt = rank(T, K * NT, E, TTR, NS, m, None)
            pool.wait(m_pos, m)
            for k in range(K):
                for t in range(NT):
                    c = k * NT + t
                    m_sc = pool.dma(lambda e, c=c, t=t: e.indirect_dma_start(
                        out=SRT[0:NS * 128, :], out_offset=bass.IndirectOffsetOnAxis(ap=pos[:, c:c + 1].bitcast(U32), axis=0),
                        in_=xs[:, t, :], in_offset=None), s_sc[0])
            if keep:
                for t in range(NT):
                    m = dve.do(lambda e, t=t: e.tensor_tensor(X[:, t, :], X[:, t, :], xs[:, t, :], ALU.add))
                dve.wait(m)
            NB = 3
            xin = region([128, NB, D])
            aT = [region([128, 2, max(1, dims[l] // 128) * 128]) for l in range(nl)]
            act_in = [region([128, 2, dims[l + 1]]) for l in range(nl)]
            yo = region([128, 4, D])
            mk, tp, tv = {}, {}, {}
            sp.wait(m_sc)
            pe.wait(m_W, m_tt)
            dve.wait(m_W, m_tt)

            def fetch(s):
                mk["in", s] = sp.dma(lambda e: e.dma_start(xin[:, s % NB, :], SRT[s * 128:(s + 1) * 128, :]),
                                     s_in[s % NB], *got(mk, "tr", s - NB, 0))

            def turn(l):
                def step(s):
                    di = dims[l]
                    src = xin[:, s % NB, :] if l == 0 else act_in[l - 1][:, s % 2, :]
                    bank = PB[l]
                    n = max(1, di // 128)
                    p = min(di, 128)

                    def tr(e):
                        for k in range(n):
                            r = e.transpose(bank[0:p, k * 128:(k + 1) * 128], src[:, k * p:(k + 1) * p], ident[:, :])
                        return r
                    m = mk["tr", s, l] = pe.do(tr, mk["in", s] if l == 0 else mk["act", s, l - 1],
                                               *got(mk, "at", s - 1, l))
                    f = ACT.Copy if l == 0 else func
                    mk["at", s, l] = act.do(lambda e: e.activation(aT[l][0:p, s % 2, :], bank[0:p, 0:n * 128], f), m,
                                            *got(mk, "mm", s - 2, l))
                return step

            def layer(l):
                def step(s):
                    if l == 0:
                        tiles_of(pe, "pe", TTR, s, 1, tp.setdefault(0, {}), s, E)
                    else:
                        tiles_of(pe, "pe", TTR, s, 1, tp.setdefault(l, {}), s, E)
                    tiles_of(dve, "dve", TTR, s, 1, tv.setdefault(l, {}), s, E)
                    di, do = dims[l], dims[l + 1]
                    n, p = max(1, di // 128), min(di, 128)
                    bank = PB[4 + l]

                    def mm(e):
                        for k in range(n):
                            r = e.matmul(bank[:, 0:do], aT[l][0:p, s % 2, k * 128:(k + 1) * 128],
                                         Ws[l][0:p, k, bass.ds(tp[l][s] * do, do)], start=(k == 0), stop=(k == n - 1))
                        return r
                    m = mk["mm", s, l] = pe.do(mm, mk["at", s, l], *got(mk, "act", s - 1, l))
                    dst = act_in[l][:, s % 2, :] if l < nl - 1 or last_relu else yo[:, s % 4, :]
                    free = got(mk, "tr", s - 2, l + 1) if l < nl - 1 else (
                        got(mk, "yo", s - 2) if last_relu else ([s_tab[s % 4].all()] if s >= 4 else []))
                    m = mk["act", s, l] = dve.do(lambda e: e.tensor_tensor(
                        dst, bank[:, 0:do], Bs[l][:, bass.ds(tv[l][s] * do, do)], ALU.add), m, *free)
                    if l == nl - 1:
                        if last_relu:
                            m = mk["yo", s] = act.do(lambda e: e.activation(yo[:, s % 4, :], act_in[l][:, s % 2, :], ACT.Relu),
                                                     m, *([s_tab[s % 4].all()] if s >= 4 else []))
                        sp.dma(lambda e: e.dma_start(OUTS[s * 128:(s + 1) * 128, :], yo[:, s % 4, :]), s_tab[s % 4], m)
                return step
            stages = []
            for l in range(nl):
                stages += [(2 * l + 3, layer(l)), (2 * l + 2, turn(l))]
            stages = sorted(stages, key=lambda x: -x[0]) + [(0, fetch)]
            pipeline(NS, stages)
            back = region([128, 4, D])
            pool.wait(*[d.all() for d in s_tab])
            n = 0
            bk = {}
            for t in range(NT):
                for k in range(K):
                    b = n % 4
                    c = k * NT + t
                    m = pool.dma(lambda e, c=c, b=b: e.indirect_dma_start(
                        out=back[:, b, :], out_offset=None, in_=OUTS[0:NS * 128, :],
                        in_offset=bass.IndirectOffsetOnAxis(ap=pos[:, c:c + 1].bitcast(U32), axis=0)),
                        s_h[b], *got(bk, n - 4))
                    if K == 1:
                        bk[n,] = dve.do(lambda e, t=t, b=b: e.tensor_tensor(X[:, t, :], X[:, t, :], back[:, b, :], ALU.add), m)
                    else:
                        bk[n,] = dve.do(lambda e, t=t, b=b, k=k: e.scalar_tensor_tensor(
                            out=X[:, t, :], in0=back[:, b, :], scalar=rw[:, k, t:t + 1], in1=X[:, t, :],
                            op0=ALU.mult, op1=ALU.add), m, *got(bk, n - 1))
                    n += 1

        def linear_router(w, b, E):
            def router(lgt, m_xnt, mz, src=None):
                per = 512 // E
                ms = []
                for q, t0 in enumerate(range(0, NT, per)):
                    t1 = min(NT, t0 + per)
                    bank = PB[2 + q]

                    def mm(e, t0=t0, t1=t1, bank=bank):
                        for t in range(t0, t1):
                            for k in range(2):
                                r = e.matmul(bank[:, (t - t0) * E:(t - t0 + 1) * E],
                                             XNT[:, k, t * 128:(t + 1) * 128], w[:, k, :],
                                             start=(k == 0), stop=(k == 1))
                        return r
                    m = pe.do(mm, m_xnt[t1 - 1], m_w_now[0])
                    pv = bank[:, 0:(t1 - t0) * E].rearrange("p (t e) -> p t e", e=E)
                    if b is None:
                        ms = dve.do(lambda e, t0=t0, t1=t1, pv=pv: e.tensor_copy(lgt[:, t0:t1, 0:E], pv), m, mz)
                    else:
                        ms = dve.do(lambda e, t0=t0, t1=t1, pv=pv: e.tensor_tensor(
                            lgt[:, t0:t1, 0:E], pv, b.unsqueeze(1).to_broadcast([128, t1 - t0, E]), ALU.add), m, mz)
                return ms
            return router

        m_w_now = [None]

        def top8(lgt, top, ix, m):
            for t in range(NT):
                m1 = dve.do(lambda e, t=t: e.max(top[:, t, :], lgt[:, t, :]), m)
            for t in range(NT):
                m2 = dve.do(lambda e, t=t: e.max_index(ix[:, t, :], top[:, t, :], lgt[:, t, :]), m1)
            return m2

        def softmax8(lgt, m, E):
            mx = region([128, NT])
            m = dve.do(lambda e: e.tensor_reduce(mx, lgt, axis=AX.X, op=ALU.max), m)
            m = dve.do(lambda e: e.tensor_tensor(lgt, lgt, mx.unsqueeze(2).to_broadcast([128, NT, 8]), ALU.subtract), m)
            m = act.do(lambda e: e.activation(lgt, lgt, ACT.Exp), m)
            m = dve.do(lambda e: e.tensor_reduce(mx, lgt, axis=AX.X, op=ALU.add), m)
            m = dve.do(lambda e: e.reciprocal(mx, mx), m)
            m = dve.do(lambda e: e.tensor_tensor(lgt, lgt, mx.unsqueeze(2).to_broadcast([128, NT, 8]), ALU.mult), m)
            if E < 8:
                m = dve.do(lambda e: e.memset(lgt[:, :, E:8], -1.0), m)
            return m

        def l0_ffn():
            w = region([128, 2, 32])
            b = region([128, 32])
            load2(w, A["L0_ffn_rwT"])
            m_w_now[0] = load_rows(b, A["L0_ffn_router_b"])
            dve.wait(m_w_now[0])

            def choose(lgt, top, ix, rw, m):
                return top8(lgt, top, ix, m)
            routed("l0", 32, 1, 56, [256, 64, 256], [A["L0_ffn_W1"], A["L0_ffn_W2"]],
                   [A["L0_ffn_b1"], A["L0_ffn_b2"]], ACT.Relu, linear_router(w, b, 32), choose, True)

        def l1_ffn():
            w1 = region([128, 2, 128])
            b1 = region([128, 1])
            w2 = region([128, 6])
            b2 = region([128, 6])
            rh = region([128, NP_])
            load2(w1, A["L1_ffn_router_w1"])
            load1(b1, A["L1_ffn_router_b1"].rearrange("(p a) -> p a", a=1))
            load1(w2, A["L1_ffn_router_w2"])
            m_w = load_rows(b2, A["L1_ffn_router_b2"])

            def router(lgt, m_xnt, mz):
                fr = {}
                mr = None
                for g in range(7):
                    n0, n1 = g * 512, min(NP_, (g + 1) * 512)
                    bank = PB[2 + g % 2]

                    def mm(e, n0=n0, n1=n1, bank=bank):
                        for k in range(2):
                            r = e.matmul(bank[:, 0:n1 - n0], w1[:, k, :], XNT[:, k, n0:n1], start=(k == 0), stop=(k == 1))
                        return r
                    m = pe.do(mm, m_xnt[n1 // 128 - 1], m_w, *got(fr, g - 2))
                    mr = fr[g,] = act.do(lambda e, n0=n0, n1=n1, bank=bank: e.activation(
                        rh[:, n0:n1], bank[:, 0:n1 - n0], ACT.Relu, bias=b1), m, m_w)

                def mm2(e):
                    for t in range(NT):
                        r = e.matmul(PB[4][:, t * 6:t * 6 + 6], rh[:, t * 128:(t + 1) * 128], w2, start=True, stop=True)
                    return r
                m = pe.do(mm2, mr)
                return dve.do(lambda e: e.tensor_tensor(lgt[:, :, 0:6], PB[4][:, 0:150].rearrange("p (t e) -> p t e", e=6),
                                                        b2.unsqueeze(1).to_broadcast([128, NT, 6]), ALU.add), m, mz, m_w)

            def choose(lgt, top, ix, rw, m):
                m = softmax8(lgt, m, 6)
                m = top8(lgt, top, ix, m)
                d = region([128, NT])
                m = dve.do(lambda e: e.tensor_tensor(d, top[:, :, 1], top[:, :, 0], ALU.subtract), m)
                m = act.do(lambda e: e.activation(rw[:, 1, :], d, ACT.Exp), m)
                m = dve.do(lambda e: e.tensor_scalar(d, rw[:, 1, :], 1.0, None, ALU.add), m)
                m = dve.do(lambda e: e.reciprocal(rw[:, 0, :], d), m)
                return dve.do(lambda e: e.tensor_tensor(rw[:, 1, :], rw[:, 1, :], rw[:, 0, :], ALU.mult), m)
            routed("l1", 6, 2, 55, [256] * 4, [A["L1_ffn_expert_w1"], A["L1_ffn_expert_w2"], A["L1_ffn_expert_w3"]],
                   [A["L1_ffn_expert_b1"], A["L1_ffn_expert_b2"], A["L1_ffn_expert_b3"]], ACT.Relu, router, choose, False)

        def l3_ffn():
            w = region([128, 2, 8])
            m_w_now[0] = load2(w, A["L3_ffn_rwT"])

            def choose(lgt, top, ix, rw, m):
                m = softmax8(lgt, m, 8)
                m = top8(lgt, top, ix, m)
                d = region([128, NT])
                m = dve.do(lambda e: e.tensor_tensor(d, top[:, :, 1], top[:, :, 0], ALU.add), m)
                m = dve.do(lambda e: e.tensor_scalar(d, d, 1e-12, None, ALU.max), m)
                m = dve.do(lambda e: e.reciprocal(d, d), m)
                return dve.do(lambda e: e.tensor_tensor(rw, top[:, :, 0:2].rearrange("p t k -> p k t"),
                                                        d.unsqueeze(1).to_broadcast([128, 2, NT]), ALU.mult), m)
            routed("l3", 8, 2, 57, [256] * 3, [A["L3_ffn_w1"], A["L3_ffn_w2"]],
                   [A["L3_ffn_b1"], A["L3_ffn_b2"]], ACT.Gelu, linear_router(w, None, 8), choose, False, keep=True)

        def l1_gnn():
            Wy = region([128, 2, 128])
            Ws = region([128, 2, 128])
            w2s = region([128, 64])
            w2v = region([128, 64])
            f1 = region([8, 64])
            f2 = region([64, 64])
            f3 = region([64, 256])
            gb = region([128, 256])
            dn = region([128, NT])
            AG = region([128, NT, 512])
            ss = region([128, 2, NT])
            base = cur[0]
            xn = region([128, 4, D])
            hb = region([128, 4, D])
            mz = dve.do(lambda e: e.memset(Wy, 0.0))
            mz = dve.do(lambda e: e.memset(Ws, 0.0))
            for W, ws, wv in ((Wy, "L1_gnn_w1_s", "L1_gnn_w1_v"), (Ws, "L1_gnn_wsc_s", "L1_gnn_wsc_v")):
                for i in range(4):
                    h, k = i % 2, i // 2
                    sp.dma(lambda e, W=W, h=h, k=k, i=i, ws=ws, wv=wv: e.dma_start(
                        W[64 * h:64 * h + 64, k, 64 * h:64 * h + 64], A[ws if i == 0 else wv]), s_w[0], mz)
            load1(w2s, A["L1_gnn_w2_s"])
            load1(w2v, A["L1_gnn_w2_v"])
            load1(f1, A["L1_gnn_fc_w1"])
            load1(f2, A["L1_gnn_fc_w2"])
            load1(f3, A["L1_gnn_w3o"])
            m_w = load_rows(gb, A["L1_gnn_g"][0, :])
            m_sc = dve.do(lambda e: e.tensor_scalar(Wy, Wy, 0.125, None, ALU.mult), m_w)
            dve.do(lambda e: e.tensor_scalar(Ws, Ws, 0.125, None, ALU.mult))
            m_f = dve.do(lambda e: e.tensor_scalar(f3, f3, 0.125, None, ALU.mult))
            m_f = dve.do(lambda e: e.tensor_scalar(f3[:, 192:256], f3[:, 192:256], 0.5773502691896258, None, ALU.mult), m_f)
            mz = dve.do(lambda e: e.memset(AG, 0.0))

            def parts(ap):
                return ap[:, 0:64], ap[:, 64:256].rearrange("p (u d) -> p d u", d=3)

            def produce(t, b, deps):
                s, v = parts(X[:, t, :])
                dve.do(lambda e: e.tensor_scalar(xn[:, b, 0:64], s, mv[:, t, 0:1], rstd[:, t:t + 1],
                                                 ALU.subtract, ALU.mult), *deps)
                return dve.do(lambda e: e.tensor_scalar(xn[:, b, 64:256].rearrange("p (d u) -> p d u", d=3), v,
                                                        mv[:, t, 0:1], rstd[:, t:t + 1], ALU.subtract, ALU.mult))
            m_xnt = transpose_tiles(produce, xn, 4, ln_stats(X))
            ev2 = {}
            for t in range(NT):
                p, b = 2 + t % 2, t % 4

                def mm(e, t=t, p=p):
                    for k in range(2):
                        r = e.matmul(PB[p][:, k * 128:(k + 1) * 128], XNT[:, k, t * 128:(t + 1) * 128], Wy[:, k, :],
                                     start=True, stop=True)
                    return r
                m1 = pe.do(mm, m_xnt[t], m_sc, *got(ev2, t - 2))
                free = [s_tab[b].all()] if s_tab[b].n else []
                m2 = ev2[t,] = act.do(lambda e, p=p, b=b: e.activation(hb[:, b, :], PB[p][:, 0:256], ACT.Copy), m1, *free)
                sp.dma(lambda e, t=t, b=b: e.dma_start(YTAB[t * 128:(t + 1) * 128, :], hb[:, b, :]), s_tab[b], m2)
            barrier()
            cur[0] = base
            GB, OB, RB = 6, 3, 12
            REC = region([128, RB, G, 16])
            Gt = region([128, GB, G, 256])
            OH = region([128, OB, G, 128])
            aT = region([8, 2, 512])
            h1 = region([64, 2, 512])
            h2 = region([64, 2, 512])
            Wt = region([128, 3, G, 256])
            M = region([128, 3, G, 512])
            tB = region([128, 2, G, 64])
            tD = region([128, G, 192])
            tS = region([128, G, 64])
            mk, tv = {("acc",): mz}, {}

            def records(g):
                mk["rec", g] = sp.dma(lambda e: e.dma_start(
                    REC[:, g % RB], RECS[g * G * 128:(g + 1) * G * 128, :].rearrange("(c p) f -> p c f", p=128)),
                    s_r[g % RB], *got(mk, "prod", g - RB), *got(mk, "oh", g - RB))

            def gather(g):
                for j in range(G):
                    mk["g", g] = pool.dma(lambda e, j=j: e.indirect_dma_start(
                        out=Gt[:, g % GB, j, :], out_offset=None, in_=YTAB,
                        in_offset=bass.IndirectOffsetOnAxis(ap=REC[:, g % RB, j, 1:2].bitcast(U32), axis=0)),
                        s_g8[g % GB], mk["rec", g], *got(mk, "prod", g - GB))

            def at_tr(g):
                def tr(e):
                    for j in range(G):
                        r = e.transpose(PB[0][0:8, j * 128:(j + 1) * 128], REC[:, g % RB, j, 6:14], ident[:, :])
                    return r
                mk["at_tr", g] = pe.do(tr, mk["rec", g], *got(mk, "at", g - 1))

            def at_ev(g):
                mk["at", g] = act.do(lambda e: e.activation(aT[:, g % 2, :], PB[0][0:8, :], ACT.Copy), mk["at_tr", g],
                                     *got(mk, "h1m", g - 2))

            def h1_mm(g):
                mk["h1m", g] = pe.do(lambda e: e.matmul(PB[1][0:64, :], f1, aT[:, g % 2, :], start=True, stop=True),
                                     mk["at", g], *got(mk, "h1", g - 1))

            def h1_ev(g):
                mk["h1", g] = act.do(lambda e: e.activation(h1[:, g % 2, :], PB[1][0:64, :], ACT.Silu, scale=8.0 ** -0.5),
                                     mk["h1m", g], *got(mk, "h2m", g - 2))

            def h2_mm(g):
                mk["h2m", g] = pe.do(lambda e: e.matmul(PB[2][0:64, :], f2, h1[:, g % 2, :], start=True, stop=True),
                                     mk["h1", g], *got(mk, "h2", g - 1))

            def h2_ev(g):
                mk["h2", g] = act.do(lambda e: e.activation(h2[:, g % 2, :], PB[2][0:64, :], ACT.Silu, scale=0.125),
                                     mk["h2m", g], *got(mk, "wm", g - 2, 1))

            def w_mm(g):
                for i in range(2):
                    def mm(e, i=i):
                        for j in range(2):
                            c = 2 * i + j
                            r = e.matmul(PB[3 + i][:, j * 256:(j + 1) * 256], h2[:, g % 2, c * 128:(c + 1) * 128], f3,
                                         start=True, stop=True)
                        return r
                    mk["wm", g, i] = pe.do(mm, mk["h2", g], *got(mk, "wt", g - 1, i))

            def w_ev(g):
                for i in range(2):
                    for j in range(2):
                        c = 2 * i + j
                        act.do(lambda e, i=i, j=j, c=c: e.activation(
                            Wt[:, g % 3, c, 0:128], PB[3 + i][:, j * 256:j * 256 + 128], ACT.Copy,
                            scale=REC[:, g % RB, c, 2:3]), mk["wm", g, i], *got(mk, "prod", g - 3))
                        mk["wt", g, i] = act.do(lambda e, i=i, j=j, c=c: e.activation(
                            Wt[:, g % 3, c, 128:256], PB[3 + i][:, j * 256 + 128:j * 256 + 256], ACT.Copy))

            def products(g):
                w, y, mm_ = Wt[:, g % 3], Gt[:, g % GB], M[:, g % 3]
                r = REC[:, g % RB]
                ys = y[:, :, 0:64]
                tb = tB[:, g % 2]
                m1 = dve.do(lambda e: e.tensor_tensor(tb, w[:, :, 128:192], ys, ALU.mult),
                            mk["wt", g, 1], mk["g", g], *got(mk, "sumg", g - 3))
                dve.do(lambda e: e.tensor_tensor(mm_[:, :, 0:64], w[:, :, 0:64], ys, ALU.mult))
                yv = y[:, :, 64:256].rearrange("p g (d u) -> p g d u", d=3)
                td = tD.rearrange("p g (d u) -> p g d u", d=3)
                for j in range(G):
                    rj = r[:, j, 3:6].unsqueeze(2).to_broadcast([128, 3, 64])
                    mv_ = mm_[:, j, 128:512].rearrange("p (d h u) -> p d h u", d=3, h=2)
                    m2 = dve.do(lambda e, j=j, rj=rj: e.tensor_tensor(td[:, j], yv[:, j], rj, ALU.mult),
                                *got(mk, "prod", g - 1))
                    dve.do(lambda e, j=j, mv_=mv_: e.tensor_tensor(
                        mv_[:, :, 1, :], w[:, j, 64:128].unsqueeze(1).to_broadcast([128, 3, 64]), yv[:, j], ALU.mult))
                    m3 = dve.do(lambda e, j=j, rj=rj, mv_=mv_: e.tensor_tensor(
                        mv_[:, :, 0, :], tb[:, j, :].unsqueeze(1).to_broadcast([128, 3, 64]), rj, ALU.mult), m1)
                m2 = dve.do(lambda e: e.tensor_tensor(tS, tD[:, :, 0:64], tD[:, :, 64:128], ALU.add), m2)
                m2 = dve.do(lambda e: e.tensor_tensor(tS, tS, tD[:, :, 128:192], ALU.add), m2)
                mk["prod", g] = dve.do(lambda e: e.tensor_tensor(mm_[:, :, 64:128], tS, w[:, :, 192:256], ALU.mult), m2)

            def sums(g):
                for j in range(G):
                    n = g * G + j
                    mk["sum", n] = pe.do(lambda e, j=j, n=n: e.matmul(
                        PB[5 + n % 3][:, :], OH[:, g % OB, j, :], M[:, g % 3, j, :], start=True, stop=True),
                        mk["prod", g], mk["oh", g], *got(mk, "added", n - 3))
                    if j == 0:
                        tiles_of(dve, "dve", TTS, g * G, G, tv, g)
                    mk["acc",] = mk["added", n] = dve.do(lambda e, n=n: e.tensor_tensor(
                        AG[:, bass.ds(tv[n], 1), :], AG[:, bass.ds(tv[n], 1), :],
                        PB[5 + n % 3][:, :].unsqueeze(1), ALU.add), mk["sum", n], mk["acc",])
                mk["oh_free", g] = mk["sumg", g] = mk["sum", g * G + G - 1]
            pipeline(NG, [(12, sums), (11, products), (10, w_ev), (9, w_mm), (8, h2_ev), (7, h2_mm), (6, h1_ev),
                          (5, h1_mm), (4, at_ev), (3, at_tr),
                          (11, onehots(mk, lambda g, j: REC[:, g % RB, j, 0:1], OH, OB, iota[:, :])),
                          (6, gather), (0, records)])
            barrier()
            cur[0] = base
            R = region([128, NT, 256])
            ab = region([128, 2, 512])
            abT = region([128, 2, 512])
            sq = region([128, 2, 256])
            m = dve.do(lambda e: e.tensor_scalar(dn, DEG[:, :], 1.0, None, ALU.max))
            m = act.do(lambda e: e.activation(dn, dn, ACT.Sqrt), m)
            m_dn = dve.do(lambda e: e.reciprocal(dn, dn), m)
            mk = {}
            for t in range(NT):
                b = t % 2
                m = dve.do(lambda e, t=t, b=b: e.tensor_scalar(ab[:, b, :], AG[:, t, :], dn[:, t:t + 1], 128.0 ** -0.5,
                                                               ALU.mult, ALU.mult), m_dn, *got(mk, "tr", t - 2))

                def tr(e, b=b):
                    for k in range(4):
                        r = e.transpose(PB[b][:, k * 128:(k + 1) * 128], ab[:, b, k * 128:(k + 1) * 128], ident[:, :])
                    return r
                m = mk["tr", t] = pe.do(tr, m, *got(mk, "ev", t - 2))
                m = mk["ev", t] = act.do(lambda e, b=b: e.activation(abT[:, b, :], PB[b][:, :], ACT.Copy), m,
                                         *got(mk, "mm", t - 2))

                def mm(e, t=t, b=b):
                    bank = PB[2 + b]
                    for k in range(2):
                        e.matmul(bank[:, k * 128:(k + 1) * 128], XNT[:, k, t * 128:(t + 1) * 128], Ws[:, k, :],
                                 start=(k == 0), stop=False)
                    for k in range(4):
                        r = e.matmul(bank[:, k * 64:(k + 1) * 64], abT[:, b, k * 128:(k + 1) * 128],
                                     w2s if k == 0 else w2v, start=False, stop=(k == 3))
                    return r
                m = mk["mm", t] = pe.do(mm, m, *got(mk, "sq", t - 2))
                m = dve.do(lambda e, t=t, b=b: e.tensor_copy(R[:, t, :], PB[2 + b][:, 0:256]), m)
                act.do(lambda e, t=t, b=b: e.activation(sq[:, 0, 0:64], R[:, t, 0:64], ACT.Square,
                                                        accum_out=ss[:, 0, t:t + 1]), m)
                mk["sq", t] = act.do(lambda e, t=t, b=b: e.activation(sq[:, 1, 0:192], R[:, t, 64:256], ACT.Square,
                                                                      accum_out=ss[:, 1, t:t + 1]), act.last())
            m = mk["sq", NT - 1]
            m1 = inv_sqrt(ss[:, 0, :], ss[:, 0, :], m, scale=1.0 / 64)
            m2 = inv_sqrt(ss[:, 1, :], ss[:, 1, :], m, scale=1.0 / 192)
            for t in range(NT):
                dve.do(lambda e, t=t: e.scalar_tensor_tensor(out=R[:, t, 0:64], in0=R[:, t, 0:64], scalar=ss[:, 0, t:t + 1],
                                                             in1=gb[:, 0:64], op0=ALU.mult, op1=ALU.mult), m1)
                m = dve.do(lambda e, t=t: e.scalar_tensor_tensor(out=R[:, t, 64:256], in0=R[:, t, 64:256],
                                                                 scalar=ss[:, 1, t:t + 1], in1=gb[:, 64:256],
                                                                 op0=ALU.mult, op1=ALU.mult), m2)
                s, v = parts(X[:, t, :])
                dve.do(lambda e, t=t, s=s: e.tensor_tensor(s, s, R[:, t, 0:64], ALU.add), m)
                dve.do(lambda e, t=t, v=v: e.tensor_tensor(v, v, R[:, t, 64:256].rearrange("p (d u) -> p d u", d=3), ALU.add))

        def maxima(mk, key, LOG, MX):
            tv = {}
            Z = region([128, 2, G, 4, 128])
            MB = region([128, 2, G, 128], BF)
            cm = region([128, 2, G, 4])

            def absent(g):
                for j in range(G):
                    mk["mb", g] = dve.do(lambda e, j=j: e.tensor_scalar(
                        MB[:, g % 2, j, :], iotab[:, :], key(g, j), NOBODY, ALU.not_equal, ALU.mult),
                        *got(mk, "z", g - 2, G - 1))

            def spread(g):
                for j in range(G):
                    for h in range(4):
                        mk["z", g, j] = act.do(lambda e, j=j, h=h: e.activation(
                            Z[:, g % 2, j, h, :], MB[:, g % 2, j, :], ACT.Identity, bias=LOG[:, g * G + j, h:h + 1]),
                            mk["mb", g], mk["log", g], *got(mk, "ztr", g - 2, j))

            def turn_over(g):
                for j in range(G):
                    def tr(e, j=j):
                        for h in range(4):
                            r = e.transpose(PB[4 + j % 2][:, h * 128:(h + 1) * 128], Z[:, g % 2, j, h, :], ident[:, :])
                        return r
                    n = g * G + j
                    mk["ztr", g, j] = pe.do(tr, mk["z", g, j], *got(mk, "cm", n - 2))
                    mk["cm", n] = dve.do(lambda e, j=j: e.tensor_reduce(
                        cm[:, g % 2, j, :], PB[4 + j % 2][:, :].rearrange("p (h n) -> p h n", h=4), axis=AX.X, op=ALU.max),
                        mk["ztr", g, j])

            def largest(g):
                tiles_of(dve, "dve", TTD, g * G, G, tv, g)
                for j in range(G):
                    mk["mx",] = dve.do(lambda e, j=j: e.tensor_tensor(
                        MX[:, bass.ds(tv[g * G + j], 1), :], MX[:, bass.ds(tv[g * G + j], 1), :],
                        cm[:, g % 2, j, :].unsqueeze(1), ALU.max), mk["cm", g * G + j], *got(mk, "mx"))
            return absent, spread, turn_over, largest

        def weighted_sums(LOG, MX, REC, TAB, ACC):
            GB, OB, TB = 7, 10, 4
            Gt = region([128, GB, G, 260])
            OH = region([128, OB, G, 128])
            OHT = region([128, TB, G * 128], BF)
            pw = region([128, 4, G * 4])
            msg = region([128, 2, G, 260])
            MX3 = region([128, 3, NT * 4 + NT * 4 % 2], BF)
            mt = region([128, NT * 4])
            mk, tp, tv = {}, {}, {}
            mk["acc",] = dve.do(lambda e: e.memset(ACC, 0.0))
            m_3 = split3([MX3[:, k, :] for k in range(3)], MX.rearrange("p t h -> p (t h)"), mt)

            def edge_max(g):
                tiles_of(pe, "pe", TTD, g * G, G, tp, g)

                def mm(e):
                    for j in range(G):
                        for k in range(3):
                            r = e.matmul(PB[2 + g % 2][:, 4 * j:4 * j + 4], OHT[:, g % TB, j * 128:(j + 1) * 128],
                                         MX3[:, k, bass.ds(tp[g * G + j] * 4, 4)], start=(k == 0), stop=(k == 2))
                    return r
                mk["em", g] = mk["oht_free", g] = pe.do(mm, mk["oht", g], m_3, *got(mk, "sub", g - 2))

            def sub(g):
                mk["sub", g] = dve.do(lambda e: e.tensor_tensor(
                    pw[:, g % 4, :], LOG[:, g * G:(g + 1) * G, :].rearrange("p c h -> p (c h)"),
                    PB[2 + g % 2][:, 0:4 * G], ALU.subtract), mk["em", g])

            def expo(g):
                mk["w", g] = act.do(lambda e: e.activation(pw[:, g % 4, :], pw[:, g % 4, :], ACT.Exp), mk["sub", g])

            def weigh(g):
                mk["msg", g] = mk["g_free", g] = dve.do(lambda e: e.tensor_tensor(
                    msg[:, g % 2].rearrange("p g (h d) -> p (g h) d", h=4),
                    Gt[:, g % GB].rearrange("p g (h d) -> p (g h) d", h=4),
                    pw[:, g % 4, :].unsqueeze(2).to_broadcast([128, 4 * G, 65]), ALU.mult),
                    mk["w", g], mk["g", g], *got(mk, "sum", g - 2))

            def total(g):
                for j in range(G):
                    mk["sum", g, j] = pe.do(lambda e, j=j: e.matmul(
                        PB[4 + j][:, 0:260], OH[:, g % OB, j, :], msg[:, g % 2, j, :], start=True, stop=True),
                        mk["msg", g], *got(mk, "added", g - 1, j))
                mk["sum", g] = mk["oh_free", g] = mk["sum", g, G - 1]

            def add(g):
                tiles_of(dve, "dve", TTD, g * G, G, tv, g)
                for j in range(G):
                    mk["acc",] = mk["added", g, j] = dve.do(lambda e, j=j: e.tensor_tensor(
                        ACC[:, bass.ds(tv[g * G + j], 1), :], ACC[:, bass.ds(tv[g * G + j], 1), :],
                        PB[4 + j][:, 0:260].unsqueeze(1), ALU.add), mk["sum", g, j], mk["acc",])
            tr, ev = turn_onehots(mk, OH, OB, OHT, TB)
            pipeline(NG, [(9, add), (8, total), (7, weigh), (6, expo), (5, sub), (4, edge_max), (3, ev), (2, tr),
                          (1, onehots(mk, lambda g, j: REC[:, g * G + j, 0:1], OH, OB, iota[:, :])),
                          (2, gathers(mk, REC, Gt, GB, TAB, s_g8, "g"))])
            A4 = ACC.rearrange("p t (h d) -> p (t h) d", h=4)
            den = region([128, NT * 4])
            den2 = region([128, NT * 4])
            m = dve.do(lambda e: e.tensor_copy(den, A4[:, :, 64]), mk["acc",])
            m = dve.do(lambda e: e.tensor_scalar(den2, den, 0.0, None, ALU.is_equal), m)
            m = dve.do(lambda e: e.tensor_tensor(den, den, den2, ALU.add), m)
            m = dve.do(lambda e: e.reciprocal(den, den), m)
            return dve.do(lambda e: e.tensor_tensor(A4, A4, den.unsqueeze(2).to_broadcast([128, NT * 4, 65]), ALU.mult), m)

        def l2_gnn():
            HN = region([128, NT, D])
            qbase = cur[0]
            Q3 = region([128, 3, NT, D], BF)
            LOG = region([128, NC, 4])
            MX = region([128, NT, 4])
            REC = region([128, NC, 2])
            cols = region([128, 4, 2])
            bo = region([128, D])
            b2 = region([128, D])
            b1c = region([128, 4])
            base = cur[0]
            W = region([128, 2, 768])
            bq = region([128, 768])
            xn = region([128, 4, D])
            kb = region([128, 4, D])
            vb = region([128, 4, 260])
            qf = region([128, 4, D])
            qt = region([128, 4, D])
            for i, n in enumerate(("g1", "be1", "g2", "be2")):
                load1(cols[:, i, :], A["L2_gnn_" + n + "c"])
            for i, n in enumerate("qkv"):
                load2(W[:, :, 256 * i:256 * i + 256], A["L2_gnn_W" + n])
                load_rows(bq[:, 256 * i:256 * i + 256], A["L2_gnn_b" + n])
            load_rows(bo, A["L2_gnn_bo"])
            load_rows(b2, A["L2_gnn_b2"])
            m_w = load1(b1c, A["L2_gnn_b1c"])
            m_rec = sp.dma(lambda e: e.dma_start(REC, RECD.rearrange("(c p) f -> p c f", p=128)), s_x[0])
            dve.do(lambda e: e.tensor_scalar(W[:, :, 0:256], W[:, :, 0:256], 0.125, None, ALU.mult), m_w)
            m_s = dve.do(lambda e: e.tensor_scalar(bq[:, 0:256], bq[:, 0:256], 0.125, None, ALU.mult))
            m_one = dve.do(lambda e: e.memset(vb.rearrange("p b (h d) -> p (b h) d", h=4)[:, :, 64:65], 1.0))
            dve.do(lambda e: e.memset(MX, NOBODY))
            m = ln_stats(X)
            pr = plain_ln(X, HN)
            for t in range(NT):
                m1 = pr(t, t, [m])
            act.wait(m_w)
            m_xnt = transpose_tiles(plain_ln(HN, xn), xn, 4, ln_stats(HN, m1), affine_evac(cols[:, 0, :], cols[:, 1, :]))
            mk = {}
            for t in range(NT):
                p = 2 + 2 * (t % 2)

                def mm(e, t=t, p=p):
                    for k in range(2):
                        e.matmul(PB[p][:, :], XNT[:, k, t * 128:(t + 1) * 128], W[:, k, 0:512], start=(k == 0), stop=(k == 1))
                    for k in range(2):
                        r = e.matmul(PB[p + 1][:, 0:256], XNT[:, k, t * 128:(t + 1) * 128], W[:, k, 512:768],
                                     start=(k == 0), stop=(k == 1))
                    return r
                m = pe.do(mm, m_xnt[t], m_s, *got(mk, t - 2))
                b = t % 4
                free = [s_tab[b].all()] if s_tab[b].n else []
                mq = dve.do(lambda e, b=b, p=p: e.tensor_tensor(qf[:, b, :], PB[p][:, 0:256], bq[:, 0:256], ALU.add), m, m_s)
                split3([Q3[:, k, t, :] for k in range(3)], qf[:, b, :], qt[:, b, :], mq)
                m1 = dve.do(lambda e, p=p, b=b: e.tensor_tensor(kb[:, b, :], PB[p][:, 256:512], bq[:, 256:512], ALU.add), *free)
                m2 = mk[t,] = dve.do(lambda e, p=p, b=b: e.tensor_tensor(
                    vb[:, b, :].rearrange("p (h d) -> p h d", h=4)[:, :, 0:64],
                    PB[p + 1][:, 0:256].rearrange("p (h d) -> p h d", h=4),
                    bq[:, 512:768].rearrange("p (h d) -> p h d", h=4), ALU.add), m_one)
                sp.dma(lambda e, t=t, b=b: e.dma_start(KTAB[t * 128:(t + 1) * 128, :], kb[:, b, :]), s_tab[b], m2)
                sp.dma(lambda e, t=t, b=b: e.dma_start(VTAB[t * 128:(t + 1) * 128, :], vb[:, b, :]), s_tab[b], m2)
            barrier()
            cur[0] = base
            GB, OB, TB = 5, 3, 3
            Gt = region([128, GB, G, 256])
            OH = region([128, OB, G, 128], BF)
            OHT = region([128, TB, G * 128], BF)
            pr_ = region([128, 2, G, 256])
            mk, tp = {}, {}

            def key(g, j):
                return REC[:, g * G + j, 0:1]

            def edge_q(i):
                def step(g):
                    if i == 0:
                        tiles_of(pe, "pe", TTD, g * G, G, tp, g)

                    def mm(e):
                        for j in range(2):
                            c = 2 * i + j
                            for k in range(3):
                                r = e.matmul(QB[i][:, j * 256:(j + 1) * 256],
                                             OHT[:, g % TB, c * 128:(c + 1) * 128],
                                             Q3[:, k, bass.ds(tp[g * G + c], 1), :].rearrange("p a n -> p (a n)"),
                                             start=(k == 0), stop=(k == 2))
                        return r
                    mk["eq", g, i] = mk["oht_free", g] = pe.do(mm, mk["oht", g], *got(mk, "qk", g - 1, i))
                return step
            QB = [PB[2], PB[3]]

            def multiply(g):
                for i in range(2):
                    mk["qk", g, i] = mk["g_free", g] = dve.do(lambda e, i=i: e.tensor_tensor(
                        pr_[:, g % 2, 2 * i:2 * i + 2, :], QB[i][:, :].rearrange("p (c n) -> p c n", c=2),
                        Gt[:, g % GB, 2 * i:2 * i + 2, :], ALU.mult), mk["eq", g, i], mk["g", g], *got(mk, "log", g - 2))

            def reduce(g):
                mk["log", g] = dve.do(lambda e: e.tensor_reduce(
                    LOG[:, g * G:(g + 1) * G, :].rearrange("p c h -> p (c h)"),
                    pr_[:, g % 2].rearrange("p c (h d) -> p (c h) d", h=4), axis=AX.X, op=ALU.add), mk["qk", g, 1])

            def free_oh(g):
                mk["oh_free", g] = mk["oht_tr", g]
            absent, spread, turn_over, largest = maxima(mk, key, LOG, MX)
            tr, ev = turn_onehots(mk, OH, OB, OHT, TB)
            pipeline(NG, [(9, largest), (8, turn_over), (7, spread), (6, absent), (6, reduce), (5, multiply),
                          (4, edge_q(0)), (4, edge_q(1)), (3, ev), (2, tr), (2, free_oh),
                          (1, onehots(mk, key, OH, OB, iotab[:, :])), (2, gathers(mk, REC, Gt, GB, KTAB, s_g8, "g"))])
            barrier()
            cur[0] = qbase
            ACC = region([128, NT, 260])
            cur[0] = base
            m = weighted_sums(LOG, MX, REC, VTAB, ACC)
            barrier()
            cur[0] = base
            Wo = region([128, 2, D])
            W1 = region([128, 2, 512])
            W2 = region([128, 4, D])
            xn = region([128, 4, D])
            hT = region([128, 2, 4, 512])
            load2(Wo, A["L2_gnn_Wo"])
            load2(W1, A["L2_gnn_W1"])
            m_w = load2(W2, A["L2_gnn_W2"])

            def produce(t, b, deps):
                return dve.do(lambda e: e.tensor_copy(
                    xn[:, b, :].rearrange("p (h d) -> p h d", h=4),
                    ACC[:, t, :].rearrange("p (h d) -> p h d", h=4)[:, :, 0:64]), *deps)
            m_xnt = transpose_tiles(produce, xn, 4, m)
            mk = {}
            for t in range(NT):
                p = 2 + t % 2
                m0 = dve.do(lambda e, t=t: e.tensor_tensor(HN[:, t, :], HN[:, t, :], bo, ALU.add))

                def mm(e, t=t, p=p):
                    for k in range(2):
                        r = e.matmul(PB[p][:, 0:256], XNT[:, k, t * 128:(t + 1) * 128], Wo[:, k, :],
                                     start=(k == 0), stop=(k == 1))
                    return r
                m = pe.do(mm, m_xnt[t], m_w, *got(mk, t - 2))
                m1 = mk[t,] = dve.do(lambda e, t=t, p=p: e.tensor_tensor(HN[:, t, :], HN[:, t, :], PB[p][:, 0:256],
                                                                         ALU.add), m, m0)
            m_xnt = transpose_tiles(plain_ln(HN, xn), xn, 4, ln_stats(HN, m1), affine_evac(cols[:, 2, :], cols[:, 3, :]))
            for t in range(NT):
                m = dve.do(lambda e, t=t: e.tensor_tensor(X[:, t, :], X[:, t, :], HN[:, t, :], ALU.add))
                m = dve.do(lambda e, t=t: e.tensor_tensor(X[:, t, :], X[:, t, :], b2, ALU.add), m)
            mk = {}

            def up(g):
                n0, n1 = g * 512, min(NP_, (g + 1) * 512)
                for c in range(4):
                    bank = PB[2 + c % 2]

                    def mm(e, c=c, bank=bank):
                        for k in range(2):
                            r = e.matmul(bank[:, 0:n1 - n0], W1[:, k, c * 128:(c + 1) * 128], XNT[:, k, n0:n1],
                                         start=(k == 0), stop=(k == 1))
                        return r
                    n = 4 * g + c
                    m = pe.do(mm, m_xnt[n1 // 128 - 1], m_w, *got(mk, "up", n - 2))
                    mk["up", n] = act.do(lambda e, c=c, bank=bank: e.activation(
                        hT[:, g % 2, c, 0:n1 - n0], bank[:, 0:n1 - n0], ACT.Relu, bias=b1c[:, c:c + 1]), m,
                        *got(mk, "down", g - 2))

            def down(g):
                for t in range(4 * g, min(NT, 4 * g + 4)):
                    bank = PB[4 + t % 2]
                    o = (t - 4 * g) * 128

                    def mm(e, bank=bank, o=o):
                        for k in range(4):
                            r = e.matmul(bank[:, 0:256], hT[:, g % 2, k, o:o + 128], W2[:, k, :],
                                         start=(k == 0), stop=(k == 3))
                        return r
                    mk["down", g] = m = pe.do(mm, mk["up", 4 * g + 3], *got(mk, "x", t - 2))
                    mk["x", t] = dve.do(lambda e, t=t, bank=bank: e.tensor_tensor(
                        X[:, t, :], X[:, t, :], bank[:, 0:256], ALU.add), m)
            dve.wait(m1)
            pipeline(7, [(1, down), (0, up)])

        def l2_ffn():
            wr = region([128, 2, 8])
            br = region([128, 8])
            lgt = region([128, NT, 8])
            par = region([128, 10, 16])
            bo = region([8, D])
            CT = region([8, NP_])
            xn = region([128, 4, D])
            W = [region([128, 2, 2, D]) for _ in range(3)]
            hT = [region([128, 2, 2, 512]) for _ in range(2)]
            load2(wr, A["L2_ffn_Wr"])
            load_rows(br, A["L2_ffn_br"])
            load1(bo, A["L2_ffn_bo"])
            names = ("b1", "g1", "be1", "m1", "v1", "b2", "g2", "be2", "m2", "v2")
            for i, n in enumerate(names):
                m_w_now[0] = load1(par[:, i, :], A["L2_ffn_" + n + "c"])
            m_w = m_w_now[0]
            dve.wait(m_w)
            m_p = []
            for o in (0, 5):
                m = inv_sqrt(par[:, o + 4, :], par[:, o + 4, :], m_w, eps_col=1)
                m = dve.do(lambda e, o=o: e.tensor_tensor(par[:, o + 4, :], par[:, o + 4, :], par[:, o + 1, :], ALU.mult), m)
                m1 = dve.do(lambda e, o=o: e.tensor_tensor(par[:, o, :], par[:, o, :], par[:, o + 3, :], ALU.subtract))
                m1 = dve.do(lambda e, o=o: e.tensor_tensor(par[:, o, :], par[:, o, :], par[:, o + 4, :], ALU.mult), m, m1)
                m_p.append(dve.do(lambda e, o=o: e.tensor_tensor(par[:, o, :], par[:, o, :], par[:, o + 2, :], ALU.add), m1))
            m_xnt = transpose_tiles(plain_ln(X, xn), xn, 4, ln_stats(X))
            m = linear_router(wr, br, 8)(lgt, m_xnt, m_w)
            m_c = softmax8(lgt, m, 8)
            mk = {}
            for t in range(NT):
                p = 4 + t % 2
                m = pe.do(lambda e, t=t, p=p: e.transpose(PB[p][0:8, 0:128], lgt[:, t, :], ident[:, :]), m_c, *got(mk, "c", t - 2))
                m = mk["c", t] = act.do(lambda e, t=t, p=p: e.activation(CT[:, t * 128:(t + 1) * 128], PB[p][0:8, 0:128], ACT.Copy), m)
                q = 6 + t % 2
                m = pe.do(lambda e, t=t, q=q: e.matmul(PB[q][:, 0:256], CT[:, t * 128:(t + 1) * 128], bo, start=True, stop=True),
                          m, *got(mk, "b", t - 2))
                mk["b", t] = dve.do(lambda e, t=t, q=q: e.tensor_tensor(X[:, t, :], X[:, t, :], PB[q][:, 0:256], ALU.add), m)
            dve.wait(mk["b", NT - 1])
            pe.wait(mk["b", NT - 1])
            act.wait(*m_p)
            mk = {}
            IT = [(x, g) for x in range(8) for g in range(7)]
            srcs = [A["L2_ffn_W1"], A["L2_ffn_W2"], A["L2_ffn_Wo"]]

            def fetch(i):
                x, g = IT[i]
                if g == 2:
                    for l in range(3):
                        mk["W", x] = sp.dma(lambda e, l=l: e.dma_start(
                            W[l][:, x % 2], srcs[l][x].rearrange("(k p) n -> p k n", p=128)), s_in[x % 2],
                            *([mk["l3", 7 * (x - 1) - 1], mk["W", x - 2]] if x > 1 else []))

            def hidden(l):
                def step(i):
                    x, g = IT[i]
                    n0, n1 = g * 512, min(NP_, (g + 1) * 512)
                    for c in range(2):
                        bank = PB[2 * l + c]

                        def mm(e, c=c, bank=bank):
                            for k in range(2):
                                src = XNT[:, k, n0:n1] if l == 0 else hT[0][:, i % 2, k, 0:n1 - n0]
                                r = e.matmul(bank[:, 0:n1 - n0], W[l][:, x % 2, k, c * 128:(c + 1) * 128], src,
                                             start=(k == 0), stop=(k == 1))
                            return r
                        m = pe.do(mm, mk["W", x], *(got(mk, "h", i, 0, 1) if l else []), *got(mk, "h", i - 1, l, c))
                        col = 2 * x + c
                        mk["mm", i, l] = m
                        mk["h", i, l, c] = act.do(lambda e, c=c, bank=bank, col=col: e.activation(
                            hT[l][:, i % 2, c, 0:n1 - n0], bank[:, 0:n1 - n0], ACT.Relu,
                            bias=par[:, 5 * l, col:col + 1], scale=par[:, 5 * l + 4, col:col + 1]), m,
                            *got(mk, "mm", i - 2, l + 1))
                return step

            def last(i):
                x, g = IT[i]
                for t in range(4 * g, min(NT, 4 * g + 4)):
                    n = i * 4 + t - 4 * g
                    bank = PB[4 + n % 4]
                    o = (t - 4 * g) * 128

                    def mm(e, bank=bank, o=o):
                        for k in range(2):
                            r = e.matmul(bank[:, 0:256], hT[1][:, i % 2, k, o:o + 128], W[2][:, x % 2, k, :],
                                         start=(k == 0), stop=(k == 1))
                        return r
                    prev = mk.get(("bank", n % 4))
                    mk["mm", i, 2] = mk["l3", i] = m = pe.do(mm, mk["h", i, 1, 1], *([prev] if prev else []))
                    mk["bank", n % 4] = mk["x", t] = dve.do(lambda e, t=t, bank=bank: e.scalar_tensor_tensor(
                        out=X[:, t, :], in0=bank[:, 0:256], scalar=lgt[:, t, x:x + 1], in1=X[:, t, :],
                        op0=ALU.mult, op1=ALU.add), m, *got(mk, "x", t))
            pipeline(len(IT), [(9, last), (8, hidden(1)), (7, hidden(0)), (0, fetch)])

        def l3_gnn():
            ED = region([128, NT, 4])
            ED3 = region([128, 3, NT * 4], BF)
            LOG = region([128, NC, 4])
            MX = region([128, NT, 4])
            REC = region([128, NC, 2])
            base = cur[0]
            Wx = region([128, 2, 264])
            WT = region([128, 2, D])
            at = region([128, 2, 2])
            AB = region([128, 2, 8])
            xn = region([128, 4, D])
            vb = region([128, 4, 260])
            es = region([128, NT, 4])
            et = region([128, NT * 4])
            load2(Wx[:, :, 0:256], A["L3_gnn_Wc"])
            load2(WT, A["L3_gnn_WT"])
            m_w = load2(at, A["L3_gnn_attT"])
            m_rec = sp.dma(lambda e: e.dma_start(REC, RECD.rearrange("(c p) f -> p c f", p=128)), s_x[0])
            m = dve.do(lambda e: e.memset(AB, 0.0))
            for h in range(4):
                k, r = h // 2, 64 * (h % 2)
                for c in range(2):
                    m1 = dve.do(lambda e, h=h, k=k, r=r, c=c: e.tensor_copy(
                        AB[r:r + 64, k, 4 * c + h:4 * c + h + 1], at[r:r + 64, k, c:c + 1]), m, m_w)

            def wa(e):
                for k in range(2):
                    for o in range(2):
                        r = e.matmul(PB[7][:, 8 * k:8 * k + 8], WT[:, o, k * 128:(k + 1) * 128], AB[:, o, :],
                                     start=(o == 0), stop=(o == 1))
                return r
            m = pe.do(wa, m1)
            m_wx = dve.do(lambda e: e.tensor_copy(Wx[:, :, 256:264], PB[7][:, 0:16].rearrange("p (k c) -> p k c", k=2)), m)
            m_one = dve.do(lambda e: e.memset(vb.rearrange("p b (h d) -> p (b h) d", h=4)[:, :, 64:65], 1.0))
            dve.do(lambda e: e.memset(MX, NOBODY))
            m_xnt = transpose_tiles(plain_ln(X, xn), xn, 4, ln_stats(X))
            mk = {}
            for t in range(NT):
                p, b = 2 + t % 2, t % 4

                def mm(e, t=t, p=p):
                    for k in range(2):
                        r = e.matmul(PB[p][:, 0:264], XNT[:, k, t * 128:(t + 1) * 128], Wx[:, k, :],
                                     start=(k == 0), stop=(k == 1))
                    return r
                m = pe.do(mm, m_xnt[t], m_wx, *(mk.get(t - 2, [])))
                free = [s_tab[b].all()] if s_tab[b].n else []
                m1 = act.do(lambda e, p=p, b=b: e.activation(
                    vb[:, b, :].rearrange("p (h d) -> p h d", h=4)[:, :, 0:64],
                    PB[p][:, 0:256].rearrange("p (h d) -> p h d", h=4), ACT.Copy), m, m_one, *free)
                dve.do(lambda e, p=p, t=t: e.tensor_copy(es[:, t, :], PB[p][:, 256:260]), m, m1)
                m2 = dve.do(lambda e, p=p, t=t: e.tensor_copy(ED[:, t, :], PB[p][:, 260:264]))
                mk[t] = [m1, m2]
                sp.dma(lambda e, t=t, b=b: e.dma_start(VTAB[t * 128:(t + 1) * 128, :], vb[:, b, :]), s_tab[b], m1)
            split3([ED3[:, k, :] for k in range(3)], ED.rearrange("p t h -> p (t h)"), et, m2)
            m2 = dve.do(lambda e: e.tensor_scalar(es[:, NT - 1, :], es[:, NT - 1, :], real[:, :], None, ALU.mult), m2)
            sp.dma(lambda e: e.dma_start(ETAB.rearrange("(t p) h -> p t h", p=128), es), s_tab[0], m2)
            barrier()
            cur[0] = base
            GB, OB, TB = 8, 3, 3
            Gt = region([128, GB, G, 4])
            OH = region([128, OB, G, 128], BF)
            OHT = region([128, TB, G * 128], BF)
            lg = region([128, 2, G, 4])
            l2 = region([128, 2, G, 4])
            l3 = region([128, 2, G, 4])
            mk, tp = {}, {}

            def key(g, j):
                return REC[:, g * G + j, 0:1]

            def edge_d(g):
                tiles_of(pe, "pe", TTD, g * G, G, tp, g)

                def mm(e):
                    for c in range(G):
                        for k in range(3):
                            r = e.matmul(PB[2 + g % 2][:, 4 * c:4 * c + 4], OHT[:, g % TB, c * 128:(c + 1) * 128],
                                         ED3[:, k, bass.ds(tp[g * G + c] * 4, 4)], start=(k == 0), stop=(k == 2))
                    return r
                mk["ed", g] = mk["oht_free", g] = pe.do(mm, mk["oht", g], *got(mk, "lg", g - 2))

            def logits(g):
                mk["lg", g] = mk["g_free", g] = dve.do(lambda e: e.tensor_tensor(
                    lg[:, g % 2], PB[2 + g % 2][:, 0:4 * G].rearrange("p (c h) -> p c h", h=4), Gt[:, g % GB], ALU.add),
                    mk["ed", g], mk["g", g])

            def leak(g):
                mk["l2", g] = dve.do(lambda e: e.scalar_tensor_tensor(
                    out=l2[:, g % 2], in0=lg[:, g % 2], scalar=0.01, in1=lg[:, g % 2], op0=ALU.mult, op1=ALU.max),
                    mk["lg", g])

            def zeros(g):
                mk["l3", g] = dve.do(lambda e: e.tensor_scalar(l3[:, g % 2], l2[:, g % 2], 0.0, -1000.0,
                                                               ALU.is_equal, ALU.mult), mk["l2", g])

            def keep(g):
                mk["log", g] = dve.do(lambda e: e.tensor_tensor(LOG[:, g * G:(g + 1) * G, :], l2[:, g % 2], l3[:, g % 2],
                                                                ALU.add), mk["l3", g])

            def free_oh(g):
                mk["oh_free", g] = mk["oht_tr", g]
            absent, spread, turn_over, largest = maxima(mk, key, LOG, MX)
            tr, ev = turn_onehots(mk, OH, OB, OHT, TB)
            pipeline(NG, [(9, largest), (8, turn_over), (7, spread), (6, absent), (6, zeros), (6, keep), (5, logits),
                          (5, leak), (4, edge_d), (3, ev), (2, tr), (2, free_oh),
                          (1, onehots(mk, key, OH, OB, iotab[:, :])), (2, gathers(mk, REC, Gt, GB, ETAB, s_g8, "g"))])
            barrier()
            cur[0] = base
            ACC = region([128, NT, 260])
            m = weighted_sums(LOG, MX, REC, VTAB, ACC)
            for t in range(NT):
                dve.do(lambda e, t=t: e.tensor_tensor(
                    X[:, t, :].rearrange("p (h d) -> p h d", h=4), X[:, t, :].rearrange("p (h d) -> p h d", h=4),
                    ACC[:, t, :].rearrange("p (h d) -> p h d", h=4)[:, :, 0:64], ALU.add), m)

        DEG = sb("DEG", [128, NT])
        sort(A["src"], A["dst"], 16, RECS, TTS, (A["edge_attr_4"], A["edge_attr_8"]))
        if stop >= 5:
            sort(A["dst"], A["src"], 2, RECD, TTD, None)
        for layer_of in (l0_gnn, l0_ffn, l1_gnn, l1_ffn, l2_gnn, l2_ffn, l3_gnn, l3_ffn)[:stop]:
            cur[0] = 0
            layer_of()
            barrier()

        for h in range(4):
            sp.dma(lambda e, h=h: e.dma_start(out[768 * h:768 * h + 768, :].rearrange("(t p) d -> p t d", p=128),
                                         X[:, 6 * h:6 * h + 6, :]), s_x[0])
        m = sp.dma(lambda e: e.dma_start(out[(NT - 1) * 128:NN, :], X[0:TAIL, NT - 1, :]), s_x[0])
        barrier()

        block = ctx.enter_context(nc.Block())

        @block.tensor
        def _(e):
            pe.run(e)

        @block.vector
        def _(e):
            dve.run(e)

        @block.scalar
        def _(e):
            act.run(e)

        @block.gpsimd
        def _(e):
            pool.run(e)

        @block.sync
        def _(e):
            sp.run(e)


def kernel(**inputs):
    import numpy as np
    import concourse.bacc as bacc
    from concourse.bass_utils import run_bass_kernel_spmd

    arr = {k: np.ascontiguousarray(v) for k, v in inputs.items()}
    arr["L0_gnn_WT"] = np.ascontiguousarray(arr["L0_gnn_W"].T)
    arr["L0_gnn_a2"] = np.ascontiguousarray(arr["L0_gnn_a"].reshape(2, 256)[::-1].T)
    c = np.ascontiguousarray

    def columns(a):
        e = a.shape[0]
        return c(a.reshape(e, 2, 128).transpose(2, 0, 1).reshape(128, 2 * e))

    arr["L0_ffn_rwT"] = c(arr["L0_ffn_router_w"].T)
    arr["L3_ffn_rwT"] = c(arr["L3_ffn_router_w"].T)
    w3 = arr["L1_gnn_fc_w3"].reshape(64, 4, 64)
    arr["L1_gnn_w3o"] = c(w3[:, [0, 2, 1, 3], :].reshape(64, 256))
    arr["L1_gnn_g"] = c(np.concatenate([arr["L1_gnn_g_s"]] + [arr["L1_gnn_g_v"]] * 3).reshape(1, 256))
    for n in ("g1", "be1", "g2", "be2"):
        arr["L2_gnn_" + n + "c"] = c(arr["L2_gnn_" + n].reshape(2, 128).T)
    arr["L2_gnn_b1c"] = c(arr["L2_gnn_b1"].reshape(4, 128).T)
    for n in ("b1", "g1", "be1", "m1", "v1", "b2", "g2", "be2", "m2", "v2"):
        arr["L2_ffn_" + n + "c"] = columns(arr["L2_ffn_" + n])
    arr["L3_gnn_Wc"] = c(arr["L3_gnn_W"].transpose(1, 0, 2).reshape(256, 256))
    arr["L3_gnn_WT"] = c(arr["L3_gnn_W"].transpose(0, 2, 1).reshape(256, 256))
    arr["L3_gnn_attT"] = c(arr["L3_gnn_att"].reshape(4, 2, 64).transpose(0, 2, 1).reshape(256, 2))
    used = list(arr)
    nc = bacc.Bacc("TRN2", target_bir_lowering=False, num_devices=1)
    arrays, A = {}, {}
    for name in used:
        a = arr[name]
        arrays["in_" + name] = a
        A[name] = nc.dram_tensor("in_" + name, a.shape, mybir.dt.from_np(a.dtype), kind="ExternalInput").ap()
    out = nc.dram_tensor("out_0", (NN, D), FP, kind="ExternalOutput").ap()
    build(nc, A, out)
    r = run_bass_kernel_spmd(nc, [arrays], core_ids=[0])
    return r.results[0]["out_0"]
```
